# Optimizing a Trainium2 kernel written in Bass

```python
import numpy as np
import jax
import jax.numpy as jnp

def _softmax(x, axis=-1):
    return jax.nn.softmax(x, axis=axis)

def _gelu(x):
    return jax.nn.gelu(x, approximate=True)

def _silu(x):
    return jax.nn.silu(x)

def _sigmoid(x):
    return jax.nn.sigmoid(x)

def _layernorm(x, axis=-1, eps=1e-05):
    m = jnp.mean(x, axis=axis, keepdims=True)
    v = jnp.var(x, axis=axis, keepdims=True)
    return (x - m) / jnp.sqrt(v + eps)

def _scatter_add(tgt, idx, src, axis=0):
    return tgt.at[idx].add(src)

def _segment_sum(src, seg, n):
    return jax.ops.segment_sum(src, seg, n)
kernel_name = 'mk_conv_preact_d2_conv_nhwc1024_r4_2fc4df'

def setup_inputs(seed: int=0):
    np.random.seed(seed)
    _w = jnp.asarray

    def _rec_inputs():
        import jax
        import jax.numpy as jnp
        _gk = jax.random.key(seed)
        x = -0.0003929 + 0.9999 * jax.random.normal(jax.random.fold_in(_gk, 1), (4, 16, 16, 256), jnp.float32)
        return x
    x = _rec_inputs()

    def _L0_conv_setup():
        import jax, jax.numpy as jnp
        import numpy as np
        import math
        NUM_HEADS = 8
        FDIM = 16
        NUM_BUCKETS = 32
        MAX_DISTANCE = 32

        def _relative_position_bucket(rel_pos, num_buckets=NUM_BUCKETS, max_distance=MAX_DISTANCE):
            nb = num_buckets // 2
            ret = (rel_pos >= 0).astype(jnp.int32) * nb
            n = jnp.abs(rel_pos)
            max_exact = nb // 2
            is_small = n < max_exact
            val_large = max_exact + (jnp.log(jnp.maximum(n, 1).astype(jnp.float32) / max_exact) / math.log(max_distance / max_exact) * (nb - max_exact)).astype(jnp.int32)
            val_large = jnp.minimum(val_large, nb - 1)
            return ret + jnp.where(is_small, n, val_large)
        key = jax.random.key(seed)
        k = jax.random.split(key, 5)
        B, Nin, F, T = (4, 16, FDIM, 256)
        N = NUM_HEADS * FDIM
        x = jax.random.normal(k[0], (B, Nin, F, T), dtype=jnp.float32)
        w_in = jax.random.normal(k[1], (NUM_HEADS, Nin), dtype=jnp.float32) / np.sqrt(Nin)
        w_qk = jax.random.normal(k[2], (2 * N, N), dtype=jnp.float32) / np.sqrt(N)
        w_out = jax.random.normal(k[3], (Nin, NUM_HEADS), dtype=jnp.float32) / np.sqrt(NUM_HEADS)
        rel_bias = jax.random.normal(k[4], (NUM_BUCKETS, NUM_HEADS), dtype=jnp.float32) * 0.02
        return {'x': x, 'w_in': w_in, 'w_qk': w_qk, 'w_out': w_out, 'rel_bias': rel_bias}
    _L0_conv_all = _L0_conv_setup()
    _L0_conv_in = {k: v for k, v in _L0_conv_all.items() if k in ('w_in', 'w_qk', 'w_out', 'rel_bias')}
    del _L0_conv_all

    def _L1_conv_setup():
        import jax, jax.numpy as jnp
        import numpy as np
        DIM = 256
        H = 16
        HD = 16
        CHUNK = 4
        key = jax.random.key(seed)
        k1, k2, k3 = jax.random.split(key, 3)
        B, F, N = (2, 32, 32)
        inner = H * HD
        x = jax.random.normal(k1, (B, F, N, DIM), dtype=jnp.float32)
        w_qkv = jax.random.normal(k2, (3 * inner, DIM), dtype=jnp.float32) * 0.02
        w_out = jax.random.normal(k3, (DIM, inner), dtype=jnp.float32) * 0.02
        return {'x': x, 'w_qkv': w_qkv, 'w_out': w_out}
    _L1_conv_all = _L1_conv_setup()
    _L1_conv_in = {k: v for k, v in _L1_conv_all.items() if k in ('w_qkv', 'w_out')}
    del _L1_conv_all
    return {'x': x, 'L0_conv_w_in': _L0_conv_in['w_in'], 'L0_conv_w_qk': _L0_conv_in['w_qk'], 'L0_conv_w_out': _L0_conv_in['w_out'], 'L0_conv_rel_bias': _L0_conv_in['rel_bias'], 'L1_conv_w_qkv': _L1_conv_in['w_qkv'], 'L1_conv_w_out': _L1_conv_in['w_out']}

def reference(x, L0_conv_w_in, L0_conv_w_qk, L0_conv_w_out, L0_conv_rel_bias, L1_conv_w_qkv, L1_conv_w_out):
    import jax
    import jax.numpy as jnp

    def _L0_conv_ref(x, w_in, w_qk, w_out, rel_bias):
        import jax, jax.numpy as jnp
        import numpy as np
        import math
        NUM_HEADS = 8
        FDIM = 16
        NUM_BUCKETS = 32
        MAX_DISTANCE = 32

        def _relative_position_bucket(rel_pos, num_buckets=NUM_BUCKETS, max_distance=MAX_DISTANCE):
            nb = num_buckets // 2
            ret = (rel_pos >= 0).astype(jnp.int32) * nb
            n = jnp.abs(rel_pos)
            max_exact = nb // 2
            is_small = n < max_exact
            val_large = max_exact + (jnp.log(jnp.maximum(n, 1).astype(jnp.float32) / max_exact) / math.log(max_distance / max_exact) * (nb - max_exact)).astype(jnp.int32)
            val_large = jnp.minimum(val_large, nb - 1)
            return ret + jnp.where(is_small, n, val_large)
        B, Nin, F, T = x.shape
        h, f = (NUM_HEADS, FDIM)
        scale = f ** (-0.5)
        xi = jnp.einsum('bcft,hc->bhft', x, w_in)
        xr = xi.reshape(B, h * f, T)
        v = xr.reshape(B, h, f, T).transpose(0, 1, 3, 2)
        qk = jnp.einsum('bct,dc->bdt', xr, w_qk)
        qk = qk.reshape(B, h, 2 * f, T).transpose(0, 1, 3, 2)
        q, k = (qk[..., :f], qk[..., f:])
        sim = jnp.einsum('bhnd,bhmd->bhnm', q, k)
        q_pos = jnp.arange(T)
        k_pos = jnp.arange(T)
        rel = k_pos[None, :] - q_pos[:, None]
        buckets = _relative_position_bucket(rel)
        bias = rel_bias[buckets]
        bias = bias.transpose(2, 0, 1)[None]
        sim = (sim + bias) * scale
        attn = jax.nn.softmax(sim, axis=-1)
        out = jnp.einsum('bhnm,bhmd->bhnd', attn, v)
        out = out.transpose(0, 1, 3, 2)
        out = jnp.einsum('bhft,ch->bcft', out, w_out)
        return out

    def _L1_conv_ref(x, w_qkv, w_out):
        import jax, jax.numpy as jnp
        import numpy as np
        DIM = 256
        H = 16
        HD = 16
        CHUNK = 4
        "Chunked frame-local attention.\n\n            For chunk i, queries of chunk i attend to keys/values of chunks\n            {i-1, i} (just {0} for i == 0). Equivalent to the torch module because\n            the qkv projection is identical across overlapping windows and only the\n            current-chunk rows of each window's output are kept.\n            "
        B, F, N, D = x.shape
        C = F // CHUNK
        L = CHUNK * N
        T = F * N
        scale = 1.0 / jnp.sqrt(jnp.asarray(HD, dtype=x.dtype))
        flat = x.reshape(B, T, D)
        qkv = flat @ w_qkv.T
        qkv = qkv.reshape(B, T, 3, H, HD)
        q, k, v = (qkv[:, :, 0], qkv[:, :, 1], qkv[:, :, 2])
        q = q.reshape(B, C, L, H, HD)
        k = k.reshape(B, C, L, H, HD)
        v = v.reshape(B, C, L, H, HD)
        zeros = jnp.zeros_like(k[:, :1])
        k_prev = jnp.concatenate([zeros, k[:, :-1]], axis=1)
        v_prev = jnp.concatenate([zeros, v[:, :-1]], axis=1)
        k_cat = jnp.concatenate([k_prev, k], axis=2)
        v_cat = jnp.concatenate([v_prev, v], axis=2)
        chunk_idx = jnp.arange(C)[:, None]
        kv_pos = jnp.arange(2 * L)[None, :]
        valid = (chunk_idx > 0) | (kv_pos >= L)
        scores = jnp.einsum('bclhd,bcmhd->bchlm', q, k_cat) * scale
        scores = jnp.where(valid[None, :, None, None, :], scores, jnp.finfo(scores.dtype).min)
        attn = jax.nn.softmax(scores, axis=-1)
        out = jnp.einsum('bchlm,bcmhd->bclhd', attn, v_cat)
        out = out.reshape(B, T, H * HD) @ w_out.T
        return out.reshape(B, F, N, D)

    def _gn(v, G=32, eps=1e-05):
        B_, H_, W_, C_ = v.shape
        g = v.reshape(B_, H_, W_, G, C_ // G)
        m = jnp.mean(g, axis=(1, 2, 4), keepdims=True)
        s = jnp.var(g, axis=(1, 2, 4), keepdims=True)
        return ((g - m) / jnp.sqrt(s + eps)).reshape(v.shape)

    def _ln_c(v, eps=1e-06):
        m = jnp.mean(v, axis=-1, keepdims=True)
        s = jnp.var(v, axis=-1, keepdims=True)
        return (v - m) / jnp.sqrt(s + eps)

    def _ln_t(v, eps=1e-05):
        m = jnp.mean(v, axis=-1, keepdims=True)
        s = jnp.var(v, axis=-1, keepdims=True)
        return (v - m) / jnp.sqrt(s + eps)

    def _to_tokens(v):
        B_, H_, W_, C_ = v.shape
        return v.reshape(B_, H_ * W_, C_)

    def _from_tokens(t, like):
        return t.reshape(like.shape)
    x = x + _L0_conv_ref(_gn(x), L0_conv_w_in, L0_conv_w_qk, L0_conv_w_out, L0_conv_rel_bias)
    x = x + _L1_conv_ref(_gn(x), L1_conv_w_qkv, L1_conv_w_out)
    return x

_drawn_inputs = setup_inputs


def setup_inputs(seed=0):
    import zlib

    import numpy as np

    out = dict(_drawn_inputs(seed))
    spreads = {}
    factors = {'L0_conv_rel_bias': 58.16, 'L1_conv_w_qkv': 5.537, 'L1_conv_w_out': 5.313}
    for name, (base, spread) in spreads.items():
        noise = np.random.default_rng([zlib.crc32(name.encode()), seed]).standard_normal(out[name].shape)
        drawn = base * np.exp(spread * noise) if base else spread * noise
        out[name] = jnp.asarray(drawn.astype(out[name].dtype))
    for name, factor in factors.items():
        out[name] = (out[name] * factor).astype(out[name].dtype)
    return out
```

```python
import math
from contextlib import ExitStack

import numpy as np

import concourse.bass as bass
from concourse import mybir

F32 = mybir.dt.float32
F32R = mybir.dt.float32r
ALU = mybir.AluOpType
ACT = mybir.ActivationFunctionType
AX = mybir.AxisListType

P = 128
BATCH, HEIGHT, WIDTH, CH = 4, 16, 16, 256
TOK = HEIGHT * WIDTH
TT = TOK // P
CT = CH // P
HD = 16
HA = 8
HB = 16
CHUNK = 4 * WIDTH
NCH = TOK // CHUNK
GRP = 32
GC = CH // GRP
EPS = 1e-5
SCALE = HD ** -0.5
NBUCKET = 32
MAXDIST = 32
UNITS = 2 * BATCH
BLK = 8
BW = 512
TOEP = CH + P
NDIAG = 512

C_ID, C_REV, C_GRP, C_SUB, C_PAR, C_LOW = 0, P, 2 * P, 3 * P, 3 * P + HD, 3 * P + HD + 2
C_END = C_LOW + 1


def shape_constants():
    p = np.arange(P)
    c = np.zeros((P, C_END), np.float32)
    c[p, C_ID + p] = 1
    c[p, C_REV + P - 1 - p] = 1
    c[:, C_GRP:C_GRP + P] = (p[:, None] // GC == p[None, :] // GC) / GC
    c[p, C_SUB + p % HD] = 1
    c[p, C_PAR + p // HD % 2] = 1
    c[:, C_LOW] = -(p // HD % 2)
    rel = 255 - np.arange(NDIAG)
    half, exact = NBUCKET // 2, NBUCKET // 4
    n = np.abs(rel)
    large = exact + (np.log(np.maximum(n, 1).astype(np.float32) / np.float32(exact))
                     / np.float32(math.log(MAXDIST / exact)) * np.float32(half - exact)).astype(np.int32)
    bucket = (rel >= 0) * half + np.where(n < exact, n, np.minimum(large, half - 1))
    return c, (np.arange(NBUCKET)[:, None] == bucket[None, :]).astype(np.float32)


def build(nc, x, w_in, w_qk, w_outa, rel_bias, w_qkv, w_outb, consts, buckets, out):
    with ExitStack() as ctx:
        def sb(name, shape, dt=F32):
            return ctx.enter_context(nc.sbuf_tensor(name, shape, dt))

        def sem(name):
            return ctx.enter_context(nc.semaphore(name))

        X = sb("X", [P, BATCH, TT, CH])
        Xn = sb("Xn", [P, BATCH, TT, CH])
        X1 = sb("X1", [P, BATCH, TT, CH])
        Xc, Sq = X1, Xn
        Part = sb("Part", [P, 2, BATCH, TT, GRP])
        Mu = sb("Mu", [P, BATCH, GRP])
        Sd = sb("Sd", [P, BATCH, GRP])
        Rs = sb("Rs", [P, BATCH, GRP])
        eps = sb("eps", [P, 1])
        avg = sb("avg", [P, P])
        con = sb("con", [P, C_END])
        idr = sb("idr", [P, P], F32R)
        revr = sb("revr", [P, P], F32R)
        hot = sb("hot", [NBUCKET, NDIAG])
        rb = sb("rb", [NBUCKET, HA])
        diag = sb("diag", [HA, NDIAG])
        Qm = sb("Qm", [P, 3, 2, 2, TOK])
        U = Qm[:].rearrange("p a b c n -> p (a b c n)").rearrange("p (h n) -> p h n", h=HA)
        Uh = sb("Uh", [P, HA, TOEP], F32R)
        Ul = sb("Ul", [P, HA, TOEP], F32R)
        win = sb("win", [HA, HEIGHT])
        wouta = sb("wouta", [HEIGHT, HA])
        wins = sb("wins", [HA, HEIGHT, WIDTH])
        woutas = sb("woutas", [HEIGHT, HA, HD])
        wqk = sb("wqk", [P, 2, P])
        WinK = sb("WinK", [P, TT, P])
        WoutK = sb("WoutK", [P, TT, P])
        WQ = sb("WQ", [P, 2, P])
        WK = sb("WK", [P, 2, P])
        WT = sb("WT", [P, CT, 3 * CH])
        WoT = sb("WoT", [P, 2, CH])
        XR = sb("XR", [P, CH])
        QH = sb("QH", [P, 2, CH], F32R)
        Qst = sb("Qst", [P, 3, 2, CH], F32R)
        KH = sb("KH", [P, 3, 2, CH], F32R)
        KL = sb("KL", [P, 3, 2, CH], F32R)
        VA = sb("VA", [P, 3, 2, HA, 32])
        XT = sb("XT", [P, CT, TOK])
        bst = sb("bst", [P, CT, 6])
        agg = sb("agg", [P, CT, 2])
        gm = sb("gm", [P, CT])
        dev = sb("dev", [P, CT])
        dsq = sb("dsq", [P, CT])
        mom = sb("mom", [P, CT])
        gve = sb("gve", [P, CT])
        mhalf = sb("mhalf", [P, CT])
        grs = sb("grs", [P, CT])
        gnb = sb("gnb", [P, CT])
        KORDER = (0, 0, 1, 2, 1, 2, 3)
        WINDOW = (0, 1, 3, 5)
        Kf = sb("Kf", [P, 3, 2, len(KORDER) * CHUNK])
        Qr = sb("Qr", [P, 2, 2, 2, 9 * CHUNK], F32R)
        Kr = sb("Kr", [P, 2, 2, TOK], F32R)
        VB = sb("VB", [P, 3, NCH, HB, 32])
        PT = sb("PT", [P, BLK, BW])
        wqkv = PT[:, 0:3, :].rearrange("p a (b c) -> p (a b) c", c=CH)
        woutb = PT[:, 3, :].rearrange("p (b c) -> p b c", c=CH)
        NM = sb("NM", [P, 2, 32])
        NT = sb("NT", [P, 2, 2, P], F32R)
        OS = sb("OS", [P, 2, BW])
        RC = sb("RC", [P, 2, 16])
        ON = sb("ON", [P, 2, 2, P])
        OT = sb("OT", [P, 2, 2, P])
        Y = sb("Y", [P, 2, CH])

        bank = [ctx.enter_context(nc.psum_tensor(f"bank{n}", [P, BW], F32)) for n in range(8)]
        S_BANK, Z_BANK, O_BANK, F_BANK, M_BANK = 0, 2, 4, 6, 7

        rows = nc.dram_tensor("bias_rows", (HA, NDIAG), F32, kind="Internal").ap()

        x_in = [sem(f"x_in{b}") for b in range(BATCH)]
        con_in, hot_in, rb_in, win_in, wouta_in = (sem(n) for n in ("con_in", "hot_in", "rb_in", "win_in", "wouta_in"))
        wqk_in, wqkv_in, woutb_in = sem("wqk_in"), sem("wqkv_in"), sem("woutb_in")
        rows_out, toep_in = sem("rows_out"), sem("toep_in")
        y_out = [sem(f"y_out{half}") for half in range(2)]
        nt_fill = sem("nt_fill")
        fills, dve_fills = sem("fills"), sem("dve_fills")
        rounded = sem("rounded")
        spread_ready = sem("spread_ready")
        small_done, small_ready = sem("small_done"), sem("small_ready")
        diag_done, diag_ready = sem("diag_done"), sem("diag_ready")
        wqk_done, wqk_ready = sem("wqk_done"), sem("wqk_ready")
        wb_done, wb_ready = sem("wb_done"), sem("wb_ready")
        uh_ready, ul_ready = sem("uh_ready"), sem("ul_ready")
        part_ready, mean_done, mu_ready = sem("part_ready"), sem("mean_done"), sem("mu_ready")
        cent_ready, cent_pool, sq_ready = sem("cent_ready"), sem("cent_pool"), sem("sq_ready")
        part2_ready, var_done, sd_ready, rs_ready = sem("part2_ready"), sem("var_done"), sem("sd_ready"), sem("rs_ready")
        xn_dve, xn_pool = sem("xn_dve"), sem("xn_pool")
        xr_done, xr_ready = sem("xr_done"), sem("xr_ready")
        q_done, k_done, v_done = sem("q_done"), sem("k_done"), sem("v_done")
        qh_ready, kh_ready, q_ready, k_ready, v_ready = (sem(n) for n in ("qh_ready", "kh_ready", "q_ready", "k_ready", "v_ready"))
        vx_ready = sem("vx_ready")
        xt_done, gm_done, gv_done, xt_ready = sem("xt_done"), sem("gm_done"), sem("gv_done"), sem("xt_ready")
        agg_ready, mom_ready, gve_ready, grs_ready, gnb_ready = (sem(n) for n in ("agg_ready", "mom_ready", "gve_ready", "grs_ready", "gnb_ready"))
        stat_step, mom_step = sem("stat_step"), sem("mom_step")
        s_done, max_ready, mt_done, mt_ready = sem("s_done"), sem("max_ready"), sem("mt_done"), sem("mt_ready")
        z_done, p_ready, pv_done, os_ready = sem("z_done"), sem("p_ready"), sem("pv_done"), sem("os_ready")
        t1_done, rc_ready, on_ready, t2_done, ot_ready, f_done = (sem(n) for n in ("t1_done", "rc_ready", "on_ready", "t2_done", "ot_ready", "f_done"))
        res_ready = sem("res_ready")

        block = ctx.enter_context(nc.Block())

        def is_a(i):
            return i < BATCH

        def halves(i):
            return i + 1 if is_a(i) else BATCH + 2 * (i - BATCH + 1)

        def grouped(t, b):
            return t[:, b].rearrange("p t (g c) -> p t g c", c=GC)

        def spread(t, b):
            return t[:, b].unsqueeze(1).unsqueeze(3).to_broadcast([P, TT, GRP, GC])

        def v_total(i):
            return i + 1 if is_a(i) else BATCH + 2 * (i - BATCH + 1)

        GROUPS = [(0, 1), (1, BATCH)]

        @block.sync
        def _(sp):
            sp.dma_start(X[:, 0], x[0].rearrange("(t p) c -> p t c", p=P)).then_inc(x_in[0], 16)
            sp.dma_start(rb[:], rel_bias).then_inc(rb_in, 16)
            sp.dma_start(hot[:], buckets).then_inc(hot_in, 16)
            for b in range(1, BATCH):
                sp.dma_start(X[:, b], x[b].rearrange("(t p) c -> p t c", p=P)).then_inc(x_in[b], 16)
            sp.wait_ge(diag_ready, 1)
            sp.dma_start(rows, diag[:]).then_inc(rows_out, 16)
            sp.wait_ge(rows_out, 16)
            sp.dma_start(U, bass.AP(rows.tensor, 0, [[1, P], [NDIAG, HA], [1, TOEP]])).then_inc(toep_in, 16)
            sp.dma_start(wqkv, w_qkv.rearrange("(a p) c -> p a c", p=P)).then_inc(wqkv_in, 16)
            sp.dma_start(woutb, w_outb.rearrange("(a p) c -> p a c", p=P)).then_inc(woutb_in, 16)
            for i in range(BATCH, UNITS):
                for cp in range(2):
                    n = halves(i - 1) + cp + 1
                    sp.wait_ge(res_ready, n)
                    sp.dma_start(out[i - BATCH, cp * P:(cp + 1) * P, :], Y[:, cp]).then_inc(y_out[cp], 16)
            for half in range(2):
                sp.wait_ge(y_out[half], 16 * BATCH)

        @block.gpsimd
        def _(pool):
            pool.dma_start(con[:], consts).then_inc(con_in, 16)
            pool.dma_start(win[:], w_in).then_inc(win_in, 16)
            pool.dma_start(wouta[:], w_outa).then_inc(wouta_in, 16)
            pool.dma_start(wqk[:], w_qk.rearrange("(a p) c -> p a c", p=P)).then_inc(wqk_in, 16)
            pool.wait_ge(win_in, 16)
            nc.gpsimd.tensor_copy(wins[:], win[:].unsqueeze(2).to_broadcast([HA, HEIGHT, WIDTH])).then_inc(spread_ready, 1)
            pool.wait_ge(wouta_in, 16)
            nc.gpsimd.tensor_copy(woutas[:], wouta[:].unsqueeze(2).to_broadcast([HEIGHT, HA, HD])).then_inc(spread_ready, 1)
            nc.gpsimd.memset(VA[:, :, :, :, HD:], 1.0).then_inc(fills, 1)
            nc.gpsimd.memset(mhalf[:], -0.5).then_inc(fills, 1)
            nc.gpsimd.memset(NT[:].bitcast(F32), 0.0).then_inc(nt_fill, 1)
            for n in range(3):
                pool.wait_ge(fills, 2 + 3 * n)
                nc.gpsimd.memset(VB[:, n, 1:, :, HD:], 1.0).then_inc(fills, 1)
                pool.wait_ge(fills, 3 + 3 * n)
                nc.gpsimd.memset(VB[0:CHUNK, n, 0, :, HD:], 1.0).then_inc(fills, 1)
                pool.wait_ge(fills, 4 + 3 * n)
                nc.gpsimd.memset(VB[CHUNK:, n, 0], 0.0).then_inc(fills, 1)
            pool.wait_ge(fills, 11)
            nc.gpsimd.memset(Qr[:].bitcast(F32), 0.0).then_inc(fills, 1)
            pool.wait_ge(mu_ready, 1)
            for b in range(1, BATCH):
                nc.gpsimd.tensor_tensor(grouped(Xc, b), grouped(X, b), spread(Mu, b), op=ALU.subtract).then_inc(cent_pool, 1)
            pool.wait_ge(rs_ready, 2)
            for b in range(1, BATCH):
                nc.gpsimd.tensor_tensor(grouped(Xn, b), grouped(Xc, b), spread(Rs, b), op=ALU.mult).then_inc(xn_pool, 1)
                if b == 1:
                    for h in range(HA):
                        pool.wait_ge(uh_ready, h + 1)
                        nc.gpsimd.tensor_tensor(Ul[:, h], U[:, h], Uh[:, h].bitcast(F32), op=ALU.subtract).then_inc(ul_ready, 1)
            for b in range(BATCH):
                i = BATCH + b
                if b:
                    pool.wait_ge(vx_ready, 3 * b)
                pool.wait_ge(gve_ready, b + 1)
                nc.gpsimd.tensor_tensor(grs[:], gve[:], mhalf[:], op=ALU.pow).then_inc(grs_ready, 1)
                pool.wait_ge(v_ready, v_total(i))
                n = b % 3
                nc.gpsimd.tensor_copy(VB[0:CHUNK, n, 0, :, 0:HD], VB[0:CHUNK, n, 1, :, 0:HD]).then_inc(vx_ready, 1)
                pool.wait_ge(vx_ready, 3 * b + 1)
                nc.gpsimd.tensor_copy(VB[0:CHUNK, n, 2, :, 0:HD], VB[0:CHUNK, n, 3, :, 0:HD]).then_inc(vx_ready, 1)
                pool.wait_ge(vx_ready, 3 * b + 2)
                nc.gpsimd.tensor_copy(VB[CHUNK:, n, 2, :, 0:HD], VB[CHUNK:, n, 1, :, 0:HD]).then_inc(vx_ready, 1)

        @block.tensor
        def _(pe):
            ident = con[:, C_ID:C_ID + P]

            pe.wait_ge(con_in, 16)
            pe.wait_ge(spread_ready, 2)
            small = bank[Z_BANK]
            for t in range(TT):
                lhs = wins[:, t * 8:(t + 1) * 8, :].rearrange("h c f -> h (c f)")
                nc.tensor.matmul(small[:, t * HA:(t + 1) * HA], lhs, con[0:HA, C_ID:C_ID + HA], start=True, stop=True)
            lhs = woutas[:].rearrange("c h f -> c (h f)")
            nc.tensor.matmul(small[:, 64:64 + HEIGHT], lhs, con[0:HEIGHT, C_ID:C_ID + HEIGHT], start=True, stop=True).then_inc(small_done, 1)
            pe.wait_ge(rb_in, 16)
            pe.wait_ge(hot_in, 16)
            nc.tensor.matmul(bank[Z_BANK + 1][0:HA, :], rb[:], hot[:], start=True, stop=True).then_inc(diag_done, 1)
            pe.wait_ge(wqk_in, 16)
            for a in range(2):
                last = nc.tensor.transpose(bank[O_BANK][:, a * P:(a + 1) * P], wqk[:, a, :], ident)
            last.then_inc(wqk_done, 1)

            def moments(g, which, ready, done):
                b0, b1 = GROUPS[g]
                pe.wait_ge(ready, g + 1)
                if g:
                    pe.wait_ge(rs_ready, 1)
                col = 256 * which
                for t in range(TT):
                    last = nc.tensor.matmul(bank[O_BANK + 1][:, col:col + (b1 - b0) * GRP], avg[:],
                                            Part[:, which, b0:b1, t, :], start=(t == 0), stop=(t == TT - 1))
                last.then_inc(done, 1)

            def wait_bank_f(i):
                if i > 0:
                    pe.wait_ge(v_ready, v_total(i - 1))

            def project_a(i, step):
                f = bank[F_BANK]
                if step == 0:
                    if i == 0:
                        pe.wait_ge(xn_dve, 1)
                        pe.wait_ge(small_ready, 2)
                    else:
                        pe.wait_ge(xn_pool, i)
                    wait_bank_f(i)
                    for t in range(TT):
                        last = nc.tensor.matmul(f[:, 0:CH], WinK[:, t, :], Xn[:, i, t, :], start=(t == 0), stop=(t == TT - 1))
                    last.then_inc(xr_done, 1)
                if step == 1:
                    if i == 0:
                        pe.wait_ge(wqk_ready, 2)
                    pe.wait_ge(xr_ready, i + 1)
                    for t in range(2):
                        last = nc.tensor.matmul(f[:, t * CH:(t + 1) * CH], WQ[:, t, :], XR[:], start=True, stop=True)
                    last.then_inc(q_done, 1)
                if step == 2:
                    pe.wait_ge(q_ready, i + 1)
                    for t in range(2):
                        last = nc.tensor.matmul(f[:, t * CH:(t + 1) * CH], WK[:, t, :], XR[:], start=True, stop=True)
                    last.then_inc(k_done, 1)
                if step == 3:
                    pe.wait_ge(k_ready, i + 1)
                    for m in range(2):
                        for t in range(TT):
                            last = nc.tensor.matmul(f[:, m * P:(m + 1) * P], Xn[:, i, t, m * P:(m + 1) * P], WinK[:, t, :],
                                                    start=(t == 0), stop=(t == TT - 1))
                    last.then_inc(v_done, 1)

            def project_b(i, step):
                b = i - BATCH
                f, m = bank[F_BANK], bank[M_BANK]
                if step == 0:
                    pe.wait_ge(res_ready, b + 1)
                    wait_bank_f(i)
                    for k in range(CT):
                        for t in range(TT):
                            last = nc.tensor.transpose(f[:, k * TOK + t * P:k * TOK + (t + 1) * P],
                                                       X1[:, b, t, k * P:(k + 1) * P], ident)
                    last.then_inc(xt_done, 1)
                if step == 1:
                    pe.wait_ge(agg_ready, b + 1)
                    pe.wait_ge(mt_ready, 2 * (i - 1))
                    nc.tensor.matmul(m[:, 0:CT], con[:, C_GRP:C_GRP + P], agg[:, :, 0], start=True, stop=True).then_inc(gm_done, 1)
                if step == 2:
                    pe.wait_ge(mom_ready, b + 1)
                    nc.tensor.matmul(m[:, 4:4 + CT], con[:, C_GRP:C_GRP + P], mom[:], start=True, stop=True).then_inc(gv_done, 1)
                if step in (3, 4):
                    if step == 3:
                        pe.wait_ge(xt_ready, b + 1)
                        if b == 0:
                            pe.wait_ge(wb_ready, 4)
                    else:
                        pe.wait_ge(qh_ready, i + 1)
                    for g in range(2):
                        for k in range(CT):
                            col = (step - 3) * CH + g * P
                            last = nc.tensor.matmul(f[:, g * TOK:(g + 1) * TOK], WT[:, k, col:col + P], XT[:, k, :],
                                                    start=(k == 0), stop=(k == CT - 1))
                    last.then_inc(q_done if step == 3 else k_done, 1)
                if step == 5:
                    pe.wait_ge(k_ready, i + 1)
                    for t in range(TT):
                        for k in range(CT):
                            last = nc.tensor.matmul(f[:, t * CH:(t + 1) * CH], XT[:, k, t * P:(t + 1) * P], WT[:, k, 2 * CH:],
                                                    start=(k == 0), stop=(k == CT - 1))
                    last.then_inc(v_done, 1)

            def scores_a(i, u):
                s = bank[S_BANK + u % 2]
                n, q, r = i % 3, u // 4, 32 * (u % 4)
                if i == 0:
                    pe.wait_ge(uh_ready, u + 1)
                for nt in range(2):
                    for mt in range(2):
                        col = (nt + 1 - mt) * P
                        nc.tensor.matmul(s[:, nt * CH + mt * P:nt * CH + (mt + 1) * P], Uh[:, u, col:col + P], revr[:],
                                         start=(nt + mt == 0), stop=False, skip_group_check=True)
                for nt in range(2):
                    last = nc.tensor.matmul(s[:, nt * CH:(nt + 1) * CH], Qst[r:r + 32, n, q, nt * P:(nt + 1) * P],
                                            KH[r:r + 32, n, q, :], start=False, stop=(nt == 1), skip_group_check=True)
                return last

            def scores_b(i, u):
                s = bank[S_BANK + u % 2]
                b = i - BATCH
                cp, r = u // 4, 32 * (u % 4)
                first = True
                for hh in range(4):
                    g, par = hh // 2, hh % 2
                    for c2 in range(2):
                        c = 2 * cp + c2
                        q0 = (1 + 2 * c - c2) * CHUNK
                        keys = Kr[r:r + 32, b % 2, g, :]
                        if c == 0:
                            rhs = keys[:, 0:CHUNK].unsqueeze(1).to_broadcast([32, 2, CHUNK])
                        else:
                            rhs = keys[:, (c - 1) * CHUNK:(c + 1) * CHUNK]
                        last = nc.tensor.matmul(s[:, hh * P:(hh + 1) * P], Qr[r:r + 32, b % 2, g, par, q0:q0 + P], rhs,
                                                start=first, stop=(hh == 3 and c2 == 1), skip_group_check=True)
                        first = False
                return last

            def shifted_a(i, u):
                z = bank[Z_BANK + u % 2]
                n, q, r = i % 3, u // 4, 32 * (u % 4)
                if i == 0:
                    pe.wait_ge(ul_ready, u + 1)
                for table in (Uh, Ul):
                    strip = table[:, u, :]
                    strip = bass.AP(strip.tensor, strip.offset, [strip.ap[0], [P, 2], [1, CH]])
                    nc.tensor.matmul(z[:], revr[:], strip, start=(table is Uh), stop=False, skip_group_check=True)
                zs = z[:].rearrange("p (s n) -> p s n", s=2)
                for nt in range(2):
                    k = u % 4 * 2 + nt
                    nc.tensor.matmul(zs[:, :, nt * P:(nt + 1) * P], idr[:, k:k + 1].to_broadcast([P, P]),
                                     NT[:, i % 2, q, :].unsqueeze(1).to_broadcast([P, 2, P]),
                                     start=False, stop=False, skip_group_check=True)
                for s in range(2):
                    mt = 1 - s
                    for keys in (KH, KL):
                        last = nc.tensor.matmul(zs[:, s, :], keys[r:r + 32, n, q, mt * P:(mt + 1) * P], Qst[r:r + 32, n, q, :],
                                                start=False, stop=(s == 1 and keys is KL), skip_group_check=True)
                return last

            def shifted_b(i, u):
                z = bank[Z_BANK + u % 2]
                b = i - BATCH
                n = b % 3
                cp, j = u // 4, u % 4
                r = 32 * j
                for hh in range(4):
                    k = 4 * j + hh
                    nc.tensor.matmul(z[:, hh * P:(hh + 1) * P], idr[:, k:k + 1].to_broadcast([P, P]),
                                     NT[:, i % 2, cp, :], start=(hh == 0), stop=False, skip_group_check=True)
                for hh in range(4):
                    g, par = hh // 2, hh % 2
                    for c2 in range(2):
                        c = 2 * cp + c2
                        lhs = Kf[r:r + 32, n, g, WINDOW[c] * CHUNK:(WINDOW[c] + 2) * CHUNK]
                        col = hh * P + c2 * CHUNK
                        last = nc.tensor.matmul(z[:, col:col + CHUNK], lhs, Qm[r:r + 32, n, par, g, c * CHUNK:(c + 1) * CHUNK],
                                                start=False, stop=(hh == 3 and c2 == 1), skip_group_check=True)
                return last

            def scores(i, u):
                idx = i * BLK + u
                if u == 0:
                    pe.wait_ge(q_ready, i + 1)
                    pe.wait_ge(k_ready, i + 1)
                if idx >= 2:
                    pe.wait_ge(max_ready, idx - 1)
                (scores_a if is_a(i) else scores_b)(i, u).then_inc(s_done, 1)

            def maxima(i, half):
                n = 8 if is_a(i) else 16
                pe.wait_ge(max_ready, i * BLK + 4 * (half + 1))
                if i + half > 0:
                    pe.wait_ge(mt_ready, 2 * i + half)
                if i + 1 >= BATCH and i + 1 < UNITS and half == 0:
                    pe.wait_ge(gve_ready, i + 1 - BATCH + 1)
                nc.tensor.transpose(bank[M_BANK][0:n, 0:P], NM[:, i % 2, half * n:(half + 1) * n], ident).then_inc(mt_done, 1)

            def shifted(i, u):
                idx = i * BLK + u
                if u % 4 == 0:
                    pe.wait_ge(mt_ready, 2 * i + u // 4 + 1)
                if idx >= 2:
                    pe.wait_ge(p_ready, idx - 1)
                (shifted_a if is_a(i) else shifted_b)(i, u).then_inc(z_done, 1)

            def values(i, half):
                o = bank[O_BANK + half]
                pe.wait_ge(p_ready, i * BLK + 4 * (half + 1))
                if half == 0:
                    if is_a(i):
                        pe.wait_ge(v_ready, v_total(i))
                        if i == 0:
                            pe.wait_ge(fills, 1)
                    else:
                        pe.wait_ge(vx_ready, 3 * (i - BATCH + 1))
                    if i == 0:
                        pe.wait_ge(wb_ready, 4)
                if i > 0:
                    if half == 0 or not is_a(i - 1):
                        pe.wait_ge(res_ready, halves(i - 1) - (0 if is_a(i - 1) else 1 - half))
                    else:
                        pe.wait_ge(ot_ready, halves(i - 1))
                if is_a(i):
                    for mt in range(2):
                        for hh in range(4):
                            last = nc.tensor.matmul(o[32 * hh:32 * hh + 32, 0:CH], VA[:, i % 3, mt, 4 * half + hh, :],
                                                    PT[:, 4 * half + hh, (1 - mt) * CH:(2 - mt) * CH],
                                                    start=(mt == 0), stop=(mt == 1))
                else:
                    for j in range(4):
                        for c2 in range(2):
                            for hh in range(4):
                                h = 8 * (hh // 2) + 2 * j + hh % 2
                                col = j * P + c2 * CHUNK
                                last = nc.tensor.matmul(o[32 * hh:32 * hh + 32, col:col + CHUNK],
                                                        VB[:, (i - BATCH) % 3, 2 * half + c2, h, :],
                                                        PT[:, 4 * half + j, hh * P + c2 * CHUNK:hh * P + (c2 + 1) * CHUNK],
                                                        start=True, stop=True)
                last.then_inc(pv_done, 1)

            def finish(i, half, step):
                n = halves(i - 1) + (half if not is_a(i) else 0) if i else 0
                o = bank[O_BANK + half]
                if step == 0:
                    if is_a(i):
                        pe.wait_ge(os_ready, 2 * (i + 1))
                        for nt in range(2):
                            for q in range(2):
                                col = (2 * nt + q) * P
                                last = nc.tensor.transpose(o[:, col:col + P], OS[:, q, nt * P:(nt + 1) * P], ident)
                    else:
                        pe.wait_ge(os_ready, 2 * i + half + 1)
                        for j in range(4):
                            last = nc.tensor.transpose(o[:, j * P:(j + 1) * P], OS[:, half, j * P:(j + 1) * P], ident)
                    last.then_inc(t1_done, 1)
                if step == 1:
                    pe.wait_ge(on_ready, n + 1)
                    t2 = bank[O_BANK + 1] if is_a(i) else o
                    for k in range(2):
                        src = ON[:, k, 0, :] if is_a(i) else ON[:, half, k, :]
                        last = nc.tensor.transpose(t2[:, k * P:(k + 1) * P], src, ident)
                    last.then_inc(t2_done, 1)
                if step == 2:
                    pe.wait_ge(ot_ready, n + 1)
                    if is_a(i):
                        for t in range(TT):
                            last = nc.tensor.matmul(o[:, t * CH:(t + 1) * CH], WoutK[:, t, :],
                                                    OT[:, 0, :, :].rearrange("p a b -> p (a b)"), start=True, stop=True)
                    else:
                        for g in range(2):
                            last = nc.tensor.matmul(o[:, 0:CH], OT[:, half, g, :], WoT[:, g, :], start=(g == 0), stop=(g == 1))
                    last.then_inc(f_done, 1)

            def weights_b():
                pe.wait_ge(wqkv_in, 16)
                pe.wait_ge(woutb_in, 16)
                pe.wait_ge(small_ready, 2)
                pe.wait_ge(diag_ready, 1)
                pe.wait_ge(wqk_ready, 2)
                pe.wait_ge(rs_ready, 2)
                for n in range(4):
                    for m in range(4):
                        if n < 3:
                            src = wqkv[:, 2 * n + m % 2, (m // 2) * P:(m // 2 + 1) * P]
                        else:
                            src = woutb[:, m % 2, (m // 2) * P:(m // 2 + 1) * P]
                        last = nc.tensor.transpose(bank[Z_BANK + n][:, m * P:(m + 1) * P], src, ident)
                    last.then_inc(wb_done, 1)

            pe.wait_ge(dve_fills, 1)
            moments(0, 0, part_ready, mean_done)
            moments(0, 1, part2_ready, var_done)
            for step in range(4):
                project_a(0, step)
            moments(1, 0, part_ready, mean_done)
            moments(1, 1, part2_ready, var_done)
            weights_b()
            pe.wait_ge(rounded, 2)
            for i in range(UNITS + 2):
                for u in range(BLK):
                    if i < UNITS:
                        scores(i, u)
                    if 0 < i <= UNITS:
                        shifted(i - 1, u)
                    if 1 < i <= UNITS + 1:
                        if u == 0:
                            values(i - 2, 1)
                        if not is_a(i - 2):
                            if u == 0:
                                finish(i - 2, 0, 2)
                            if 1 <= u <= 3:
                                finish(i - 2, 1, u - 1)
                        elif 1 <= u <= 3:
                            finish(i - 2, 0, u - 1)
                    if i + 1 < BATCH and u in (0, 2, 4, 6):
                        project_a(i + 1, u // 2)
                    if BATCH <= i + 1 < UNITS and u in (0, 2, 3, 5, 6, 7):
                        project_b(i + 1, (0, 2, 3, 5, 6, 7).index(u))
                    if 0 < i <= UNITS and u == 1:
                        maxima(i - 1, 1)
                    if 0 < i <= UNITS:
                        if u == 5:
                            values(i - 1, 0)
                        if not is_a(i - 1) and u in (6, 7):
                            finish(i - 1, 0, u - 6)
                    if i < UNITS and u == 5:
                        maxima(i, 0)

        @block.vector
        def _(dve):
            V = nc.vector
            V.memset(avg[:], 1.0 / (TOK * GC)).then_inc(dve_fills, 1)
            V.memset(eps[:], EPS).then_inc(dve_fills, 1)

            def part_sums(g, src, which, done):
                b0, b1 = GROUPS[g]
                V.tensor_reduce(Part[:, which, b0:b1].rearrange("p b t g -> p (b t g)"),
                                src[:, b0:b1].rearrange("p b t (g c) -> p (b t g) c", c=GC), AX.X, ALU.add).then_inc(done, 1)

            def norm_x(g, step):
                b0, b1 = GROUPS[g]
                m = bank[O_BANK + 1]
                if step == 0:
                    for b in range(b0, b1):
                        dve.wait_ge(x_in[b], 16)
                    part_sums(g, X, 0, part_ready)
                if step == 1:
                    dve.wait_ge(mean_done, g + 1)
                    if g == 0:
                        mean = m[:, 0:GRP].unsqueeze(1).unsqueeze(3).to_broadcast([P, TT, GRP, GC])
                        V.tensor_tensor(grouped(Xc, 0), grouped(X, 0), mean, op=ALU.subtract).then_inc(cent_ready, 1)
                    else:
                        V.tensor_copy(Mu[:, b0:b1].rearrange("p b g -> p (b g)"), m[:, 0:(b1 - b0) * GRP]).then_inc(mu_ready, 1)
                if step == 2:
                    dve.wait_ge(sq_ready, b1)
                    part_sums(g, Sq, 1, part2_ready)
                if step == 3:
                    dve.wait_ge(sd_ready, g + 1)
                    V.reciprocal(Rs[:, b0:b1], Sd[:, b0:b1]).then_inc(rs_ready, 1)
                    if g == 0:
                        dve.wait_ge(rs_ready, 1)
                        V.tensor_tensor(grouped(Xn, 0), grouped(Xc, 0), spread(Rs, 0), op=ALU.mult).then_inc(xn_dve, 1)

            def small_weights():
                dve.wait_ge(con_in, 16)
                dve.wait_ge(small_done, 1)
                sub = con[:, C_SUB:C_SUB + HD]
                small = bank[Z_BANK]
                V.tensor_tensor(WinK[:].rearrange("p t (h f) -> p (t h) f", f=HD),
                                small[:, 0:TT * HA].unsqueeze(2).to_broadcast([P, TT * HA, HD]),
                                sub.unsqueeze(1).to_broadcast([P, TT * HA, HD]), op=ALU.mult).then_inc(small_ready, 1)
                V.tensor_tensor(WoutK[:].rearrange("p t (c f) -> p (t c) f", f=WIDTH),
                                small[:, 64:64 + HEIGHT].unsqueeze(2).to_broadcast([P, HEIGHT, WIDTH]),
                                sub.unsqueeze(1).to_broadcast([P, HEIGHT, WIDTH]), op=ALU.mult).then_inc(small_ready, 1)
                dve.wait_ge(wqk_done, 1)
                for k, w in enumerate((WQ, WK)):
                    src = bank[O_BANK][:, 0:2 * P].rearrange("p (h k d) -> p h k d", k=2, d=HD)[:, :, k, :]
                    V.tensor_copy(w[:].rearrange("p t (h r d) -> p (t h) r d", r=2, d=HD),
                                  src.unsqueeze(2).to_broadcast([P, HA, 2, HD])).then_inc(wqk_ready, 1)

            def queries_keys(i, which):
                f = bank[F_BANK]
                if is_a(i):
                    if which == 0:
                        if i >= 3:
                            dve.wait_ge(z_done, BLK * (i - 2))
                        dve.wait_ge(qh_ready, i + 1)
                        V.scalar_tensor_tensor(Qst[:, i % 3].rearrange("p t n -> p (t n)"),
                                               QH[:].rearrange("p t n -> p (t n)").bitcast(F32), con[:, C_LOW:C_LOW + 1], f[:],
                                               ALU.mult, ALU.add).then_inc(q_ready, 1)
                    else:
                        dve.wait_ge(kh_ready, i + 1)
                        V.tensor_tensor(KL[:, i % 3].rearrange("p t n -> p (t n)"), f[:],
                                        KH[:, i % 3].rearrange("p t n -> p (t n)").bitcast(F32), op=ALU.subtract).then_inc(k_ready, 1)
                else:
                    b = i - BATCH
                    if which == 0:
                        dve.wait_ge(qh_ready, i + 1)
                        if b == 0:
                            dve.wait_ge(fills, 12)
                        if b >= 2:
                            dve.wait_ge(s_done, BLK * (i - 1))
                        for g in range(2):
                            dst = Qr[:, b % 2, g, :, CHUNK:].rearrange("p a (c z) -> p a c z", c=NCH)[:, :, :, 0:CHUNK]
                            src = Qm[:, b % 3, :, g, :].rearrange("p a (c q) -> p a c q", c=NCH)
                            last = V.tensor_copy(dst, src)
                        last.then_inc(q_ready, 1)
                    else:
                        dve.wait_ge(kh_ready, i + 1)
                        if b >= 2:
                            dve.wait_ge(s_done, BLK * (i - 1))
                        V.tensor_copy(Kr[:, b % 2].rearrange("p g n -> p (g n)"), f[:]).then_inc(k_ready, 1)

            def value_rows(i):
                f = bank[F_BANK]
                dve.wait_ge(v_done, i + 1)
                if is_a(i):
                    if i >= 3:
                        dve.wait_ge(pv_done, 2 * (i - 2))
                    V.tensor_copy(VA[:, i % 3, :, :, 0:HD], f[:, 0:2 * P].rearrange("p (m h d) -> p m h d", m=2, d=HD)).then_inc(v_ready, 1)
                else:
                    b = i - BATCH
                    if b == 0:
                        dve.wait_ge(fills, 11)
                    if b >= 3:
                        dve.wait_ge(pv_done, 2 * (i - 2))
                        dve.wait_ge(vx_ready, 3 * (b - 2))
                    for t in range(TT):
                        V.tensor_copy(VB[:, b % 3, 2 * t + 1, :, 0:HD],
                                      f[:, t * CH:(t + 1) * CH].rearrange("p (h d) -> p h d", d=HD)).then_inc(v_ready, 1)

            def norm_b(b, step):
                m = bank[M_BANK]
                c0 = 4 * b
                if step == 0:
                    dve.wait_ge(xt_done, b + 1)
                    for k in range(CT):
                        V.bn_stats(bst[:, k, :], bank[F_BANK][:, k * TOK:(k + 1) * TOK]).then_inc(stat_step, 1)
                    dve.wait_ge(stat_step, c0 + 2)
                    if b:
                        dve.wait_ge(gm_done, b)
                    for k in range(CT):
                        last = V.bn_aggr(agg[:, k, :], bst[:, k, :])
                    last.then_inc(agg_ready, 1)
                if step == 1:
                    dve.wait_ge(gm_done, b + 1)
                    V.tensor_copy(gm[:], m[:, 0:CT]).then_inc(stat_step, 1)
                    dve.wait_ge(agg_ready, b + 1)
                    dve.wait_ge(stat_step, c0 + 3)
                    V.tensor_tensor(dev[:], agg[:, :, 0], gm[:], op=ALU.subtract).then_inc(stat_step, 1)
                    dve.wait_ge(stat_step, c0 + 4)
                    V.tensor_tensor(dsq[:], dev[:], dev[:], op=ALU.mult).then_inc(mom_step, 1)
                    dve.wait_ge(mom_step, b + 1)
                    V.tensor_tensor(mom[:], dsq[:], agg[:, :, 1], op=ALU.add).then_inc(mom_ready, 1)
                if step == 2:
                    dve.wait_ge(gv_done, b + 1)
                    V.tensor_scalar(gve[:], m[:, 4:4 + CT], EPS, None, ALU.add).then_inc(gve_ready, 1)
                if step == 3:
                    dve.wait_ge(grs_ready, b + 1)
                    V.scalar_tensor_tensor(gnb[:], gm[:], -1.0, grs[:], ALU.mult, ALU.mult).then_inc(gnb_ready, 1)

            def block_max(i, u):
                dve.wait_ge(s_done, i * BLK + u + 1)
                s = bank[S_BANK + u % 2]
                if i >= 2 and u % 4 == 0:
                    dve.wait_ge(mt_done, 2 * (i - 2) + u // 4 + 1)
                if is_a(i):
                    V.tensor_reduce(NM[:, i % 2, 2 * u:2 * u + 2], s[:].rearrange("p (n m) -> p n m", n=2), AX.X, ALU.max).then_inc(max_ready, 1)
                else:
                    V.tensor_reduce(NM[:, i % 2, 4 * u:4 * u + 4], s[:].rearrange("p (h m) -> p h m", h=4), AX.X, ALU.max).then_inc(max_ready, 1)

            def divide(i, half):
                n = (halves(i - 1) if i else 0) + (0 if is_a(i) else half)
                o = bank[O_BANK + half]
                dve.wait_ge(t1_done, n + 1)
                V.reciprocal(RC[:, half, :], o[:].rearrange("p (a z) -> p a z", z=32)[:, :, HD]).then_inc(rc_ready, 1)
                dve.wait_ge(rc_ready, n + 1)
                if is_a(i):
                    V.tensor_tensor(ON[:, :, 0, :].rearrange("p n (h d) -> p n h d", d=HD),
                                    o[:].rearrange("p (n h z) -> p n h z", n=2, z=32)[:, :, :, 0:HD],
                                    RC[:, half, :].rearrange("p (n h) -> p n h", n=2).unsqueeze(3).to_broadcast([P, 2, HA, HD]),
                                    op=ALU.mult).then_inc(on_ready, 1)
                else:
                    for g in range(2):
                        last = V.tensor_tensor(
                            ON[:, half, g, :].rearrange("p (j a d) -> p j a d", j=4, d=HD),
                            o[:].rearrange("p (j g a z) -> p j g a z", j=4, g=2, z=32)[:, :, g, :, 0:HD],
                            RC[:, half, :].rearrange("p (j g a) -> p j g a", j=4, g=2)[:, :, g, :].unsqueeze(3).to_broadcast([P, 4, 2, HD]),
                            op=ALU.mult)
                    last.then_inc(on_ready, 1)

            def residual(i, half):
                n = (halves(i - 1) if i else 0) + (0 if is_a(i) else half)
                o = bank[O_BANK + half]
                dve.wait_ge(f_done, n + 1)
                if is_a(i):
                    V.tensor_tensor(X1[:, i].rearrange("p t c -> p (t c)"), o[:], X[:, i].rearrange("p t c -> p (t c)"),
                                    op=ALU.add).then_inc(res_ready, 1)
                else:
                    b = i - BATCH
                    if b:
                        dve.wait_ge(y_out[half], 16 * b)
                    V.tensor_tensor(Y[:, half], o[:, 0:CH], X1[:, b, half, :], op=ALU.add).then_inc(res_ready, 1)

            norm_x(0, 0)
            norm_x(1, 0)
            small_weights()
            dve.wait_ge(diag_done, 1)
            V.tensor_copy(diag[:], bank[Z_BANK + 1][0:HA, :]).then_inc(diag_ready, 1)
            norm_x(0, 1)
            norm_x(0, 2)
            norm_x(0, 3)
            V.tensor_copy(revr[:], con[:, C_REV:C_REV + P]).then_inc(rounded, 1)
            V.tensor_copy(idr[:], con[:, C_ID:C_ID + P]).then_inc(rounded, 1)
            queries_keys(0, 0)
            queries_keys(0, 1)
            value_rows(0)
            norm_x(1, 1)
            norm_x(1, 2)
            norm_x(1, 3)
            for i in range(UNITS + 2):
                for u in range(BLK):
                    if i < UNITS:
                        block_max(i, u)
                    if 1 < i <= UNITS + 1:
                        if not is_a(i - 2):
                            if u == 0:
                                residual(i - 2, 0)
                            if u == 1:
                                divide(i - 2, 1)
                            if u == 3:
                                residual(i - 2, 1)
                        else:
                            if u == 1:
                                divide(i - 2, 0)
                            if u == 3:
                                residual(i - 2, 0)
                    if i + 1 < BATCH:
                        if u == 2:
                            queries_keys(i + 1, 0)
                        if u == 4:
                            queries_keys(i + 1, 1)
                        if u == 6:
                            value_rows(i + 1)
                    if BATCH <= i + 1 < UNITS:
                        if u in (0, 2, 3):
                            norm_b(i + 1 - BATCH, (0, 2, 3).index(u))
                        if u == 4:
                            norm_b(i + 1 - BATCH, 3)
                        if u == 5:
                            queries_keys(i + 1, 0)
                        if u == 6:
                            queries_keys(i + 1, 1)
                        if u == 7:
                            value_rows(i + 1)
                    if 0 < i <= UNITS and not is_a(i - 1) and u == 6:
                        divide(i - 1, 0)

        @block.scalar
        def _(act):
            A = nc.scalar
            act.wait_ge(dve_fills, 2)
            act.wait_ge(nt_fill, 1)

            def squares(g):
                b0, b1 = GROUPS[g]
                for b in range(b0, b1):
                    if g == 0:
                        act.wait_ge(cent_ready, 1)
                    else:
                        act.wait_ge(cent_pool, b)
                    A.activation(Sq[:, b], Xc[:, b], ACT.Square).then_inc(sq_ready, 1)

            def deviation(g):
                b0, b1 = GROUPS[g]
                act.wait_ge(var_done, g + 1)
                A.activation(Sd[:, b0:b1].rearrange("p b g -> p (b g)"), bank[O_BANK + 1][:, 256:256 + (b1 - b0) * GRP],
                             ACT.Sqrt, bias=eps[:]).then_inc(sd_ready, 1)

            def weights_b(n):
                act.wait_ge(wb_done, n + 1)
                src = bank[Z_BANK + n][:].rearrange("p (k r) -> p k r", k=2)
                dst = WT[:, :, n * CH:(n + 1) * CH] if n < 3 else WoT[:]
                A.activation(dst, src, ACT.Copy).then_inc(wb_ready, 1)

            def projected(i, which):
                f = bank[F_BANK]
                if is_a(i):
                    if which == 0:
                        act.wait_ge(xr_done, i + 1)
                        if i:
                            act.wait_ge(k_done, i)
                        A.activation(XR[:], f[:, 0:CH], ACT.Copy).then_inc(xr_ready, 1)
                    if which == 1:
                        act.wait_ge(q_done, i + 1)
                        if i:
                            act.wait_ge(q_ready, i)
                        A.activation(QH[:].rearrange("p t n -> p (t n)"), f[:], ACT.Copy).then_inc(qh_ready, 1)
                    if which == 2:
                        act.wait_ge(k_done, i + 1)
                        if i >= 3:
                            act.wait_ge(z_done, BLK * (i - 2))
                        A.activation(KH[:, i % 3].rearrange("p t n -> p (t n)"), f[:], ACT.Copy).then_inc(kh_ready, 1)
                else:
                    b = i - BATCH
                    if which == 0:
                        act.wait_ge(gnb_ready, b + 1)
                        for k in range(CT):
                            last = A.activation(XT[:, k, :], f[:, k * TOK:(k + 1) * TOK], ACT.Identity,
                                                bias=gnb[:, k:k + 1], scale=grs[:, k:k + 1])
                        last.then_inc(xt_ready, 1)
                    if which == 1:
                        act.wait_ge(q_done, i + 1)
                        if b >= 3:
                            act.wait_ge(z_done, BLK * (i - 2))
                        for par in range(2):
                            last = A.activation(Qm[:, b % 3, par].rearrange("p g n -> p (g n)"), f[:], ACT.Copy,
                                                scale=con[:, C_PAR + par:C_PAR + par + 1])
                        last.then_inc(qh_ready, 1)
                    if which == 2:
                        act.wait_ge(k_done, i + 1)
                        if b >= 3:
                            act.wait_ge(z_done, BLK * (i - 2))
                        src = f[:].rearrange("p (g n) -> p g n", g=2)
                        for slot, c, m in ((0, 0, 1), (1, 0, 3), (4, 1, 3)):
                            last = A.activation(Kf[:, b % 3, :, slot * CHUNK:(slot + m) * CHUNK],
                                                src[:, :, c * CHUNK:(c + m) * CHUNK], ACT.Copy)
                        last.then_inc(kh_ready, 1)

            def maxima(i, half):
                n = 8 if is_a(i) else 16
                act.wait_ge(mt_done, 2 * i + half + 1)
                if i >= 2:
                    act.wait_ge(z_done, BLK * (i - 2) + 4 * (half + 1))
                A.activation(NT[0:n, i % 2, half, :], bank[M_BANK][0:n, 0:P], ACT.Copy, scale=-1.0).then_inc(mt_ready, 1)

            def probabilities(i, u):
                act.wait_ge(z_done, i * BLK + u + 1)
                if i >= 1 and u % 4 == 0:
                    act.wait_ge(pv_done, 2 * (i - 1) + u // 4 + 1)
                A.activation(PT[:, u, :], bank[Z_BANK + u % 2][:], ACT.Exp, scale=SCALE).then_inc(p_ready, 1)

            def unnormalised(i, half):
                act.wait_ge(pv_done, 2 * i + half + 1)
                if i:
                    act.wait_ge(t1_done, halves(i - 1) - (0 if is_a(i - 1) else 1 - half))
                w = CH if is_a(i) else BW
                A.activation(OS[:, half, 0:w], bank[O_BANK + half][:, 0:w], ACT.Copy).then_inc(os_ready, 1)

            def normalised(i, half):
                n = (halves(i - 1) if i else 0) + (0 if is_a(i) else half)
                t2 = bank[O_BANK + 1] if is_a(i) else bank[O_BANK + half]
                act.wait_ge(t2_done, n + 1)
                if i:
                    act.wait_ge(f_done, halves(i - 1) - (0 if is_a(i - 1) else 1 - half))
                A.activation(OT[:, 0 if is_a(i) else half].rearrange("p a b -> p (a b)"), t2[:, 0:2 * P], ACT.Copy).then_inc(ot_ready, 1)

            squares(0)
            deviation(0)
            for which in range(3):
                projected(0, which)
            squares(1)
            deviation(1)
            act.wait_ge(toep_in, 16)
            for h in range(HA):
                A.activation(Uh[:, h], U[:, h], ACT.Copy).then_inc(uh_ready, 1)
            for n in range(4):
                weights_b(n)
            for i in range(UNITS + 2):
                for u in range(BLK):
                    if 0 < i <= UNITS:
                        probabilities(i - 1, u)
                    if 1 < i <= UNITS + 1:
                        if u == 0:
                            unnormalised(i - 2, 1)
                        if u == 2:
                            normalised(i - 2, 0 if is_a(i - 2) else 1)
                    if i + 1 < BATCH and u in (0, 2, 4):
                        projected(i + 1, u // 2)
                    if BATCH <= i + 1 < UNITS and u in (4, 5, 6):
                        projected(i + 1, u - 4)
                    if 0 < i <= UNITS:
                        if u == 1:
                            maxima(i - 1, 1)
                        if u == 5:
                            unnormalised(i - 1, 0)
                        if not is_a(i - 1) and u == 7:
                            normalised(i - 1, 0)
                    if i < UNITS and u == 5:
                        maxima(i, 0)


def kernel(x, L0_conv_w_in, L0_conv_w_qk, L0_conv_w_out, L0_conv_rel_bias, L1_conv_w_qkv, L1_conv_w_out):
    import concourse.bacc as bacc
    from concourse.bass_utils import run_bass_kernel_spmd

    nc = bacc.Bacc("TRN2", target_bir_lowering=False, num_devices=1)
    consts, buckets = shape_constants()
    given = {
        "x": np.ascontiguousarray(x).reshape(BATCH, TOK, CH), "w_in": L0_conv_w_in, "w_qk": L0_conv_w_qk,
        "w_outa": L0_conv_w_out, "rel_bias": L0_conv_rel_bias, "w_qkv": L1_conv_w_qkv, "w_outb": L1_conv_w_out,
        "consts": consts, "buckets": buckets,
    }
    arrays = {name: np.ascontiguousarray(a) for name, a in given.items()}
    aps = {name: nc.dram_tensor(name, a.shape, mybir.dt.from_np(a.dtype), kind="ExternalInput").ap() for name, a in arrays.items()}
    out = nc.dram_tensor("y", (BATCH, TOK, CH), F32, kind="ExternalOutput").ap()
    build(nc, out=out, **aps)
    r = run_bass_kernel_spmd(nc, [arrays], core_ids=[0])
    return r.results[0]["y"].reshape(BATCH, HEIGHT, WIDTH, CH)
```

```python
import math
from contextlib import ExitStack

import numpy as np

import concourse.bass as bass
from concourse import mybir

F32 = mybir.dt.float32
F32R = mybir.dt.float32r
ALU = mybir.AluOpType
ACT = mybir.ActivationFunctionType
AX = mybir.AxisListType

P = 128
BATCH, HEIGHT, WIDTH, CH = 4, 16, 16, 256
TOK = HEIGHT * WIDTH
TT = TOK // P
CT = CH // P
HD = 16
HA = 8
HB = 16
CHUNK = 4 * WIDTH
NCH = TOK // CHUNK
GRP = 32
GC = CH // GRP
EPS = 1e-5
SCALE = HD ** -0.5
NBUCKET = 32
MAXDIST = 32
UNITS = 2 * BATCH
BLK = 8
BW = 512
TOEP = CH + P
NDIAG = 512

C_ID, C_REV, C_GRP, C_SUB, C_HEAD, C_LOW = 0, P, 2 * P, 3 * P, 3 * P + HD, 3 * P + HD + 8
C_END = C_LOW + 1


def shape_constants():
    p = np.arange(P)
    c = np.zeros((P, C_END), np.float32)
    c[p, C_ID + p] = 1
    c[p, C_REV + P - 1 - p] = 1
    c[:, C_GRP:C_GRP + P] = (p[:, None] // GC == p[None, :] // GC) / GC
    c[p, C_SUB + p % HD] = 1
    c[p, C_HEAD + p // HD] = 1
    c[:, C_LOW] = -(p // HD % 2)
    rel = 255 - np.arange(NDIAG)
    half, exact = NBUCKET // 2, NBUCKET // 4
    n = np.abs(rel)
    large = exact + (np.log(np.maximum(n, 1).astype(np.float32) / np.float32(exact))
                     / np.float32(math.log(MAXDIST / exact)) * np.float32(half - exact)).astype(np.int32)
    bucket = (rel >= 0) * half + np.where(n < exact, n, np.minimum(large, half - 1))
    return c, (np.arange(NBUCKET)[:, None] == bucket[None, :]).astype(np.float32)


def build(nc, x, w_in, w_qk, w_outa, rel_bias, w_qkv, w_outb, consts, buckets, out):
    with ExitStack() as ctx:
        def sb(name, shape, dt=F32):
            return ctx.enter_context(nc.sbuf_tensor(name, shape, dt))

        def sem(name):
            return ctx.enter_context(nc.semaphore(name))

        X = sb("X", [P, BATCH, TT, CH])
        Xn = sb("Xn", [P, BATCH, TT, CH])
        X1 = sb("X1", [P, BATCH, TT, CH])
        Xc, Sq = X1, Xn
        Part = sb("Part", [P, 2, BATCH, TT, GRP])
        Mu = sb("Mu", [P, BATCH, GRP])
        Sd = sb("Sd", [P, BATCH, GRP])
        Rs = sb("Rs", [P, BATCH, GRP])
        eps = sb("eps", [P, 1])
        avg = sb("avg", [P, P])
        con = sb("con", [P, C_END])
        minus = sb("minus", [P, P], F32R)
        revr = sb("revr", [P, P], F32R)
        rb = sb("rb", [NBUCKET, HA])
        Km = sb("Km", [P, 2, 8, TOK], F32R)
        Uh = sb("Uh", [P, HA, TOEP], F32R)
        Ul = sb("Ul", [P, HA, TOEP], F32R)
        win = sb("win", [HA, HEIGHT])
        wouta = sb("wouta", [HEIGHT, HA])
        wins = sb("wins", [HA, HEIGHT, WIDTH])
        woutas = sb("woutas", [HEIGHT, HA, HD])
        wqk = sb("wqk", [P, 2, P])
        WinK = sb("WinK", [P, TT, P])
        WoutK = sb("WoutK", [P, TT, P])
        WQ = sb("WQ", [P, 2, P])
        WK = sb("WK", [P, 2, P])
        WT = sb("WT", [P, CT, 3 * CH])
        WoT = sb("WoT", [P, 2, CH])
        XR = sb("XR", [P, CH])
        QH = sb("QH", [P, 2, CH], F32R)
        Qst = sb("Qst", [P, 3, 2, CH], F32R)
        KH = sb("KH", [P, 3, 2, CH], F32R)
        KL = sb("KL", [P, 3, 2, CH], F32R)
        VA = sb("VA", [P, 3, 2, HA, 32])
        XT = sb("XT", [P, CT, TOK])
        bst = sb("bst", [P, CT, 6])
        agg = sb("agg", [P, CT, 2])
        gm = sb("gm", [P, CT])
        dev = sb("dev", [P, CT])
        dsq = sb("dsq", [P, CT])
        mom = sb("mom", [P, CT])
        gve = sb("gve", [P, CT])
        mhalf = sb("mhalf", [P, CT])
        grs = sb("grs", [P, CT])
        gnb = sb("gnb", [P, CT])
        KORDER = (0, 0, 1, 2, 3, 2, 1)
        WINDOW = (0, 1, 5, 3)
        Kf = sb("Kf", [P, 3, 2, len(KORDER) * CHUNK])
        Qn = sb("Qn", [P, 3, 2, TOK])
        Qs = sb("Qs", [P, 2, 2, 2, 3, CHUNK], F32R)
        QRING = 3
        Qk = sb("Qk", [P, QRING, BW])
        VB = sb("VB", [P, 3, NCH, HB, 32])
        U = VB[:, 1:3].rearrange("p a b c n -> p (a b c n)")[:, 0:HA * TOEP].rearrange("p (h n) -> p h n", h=HA)
        PT = sb("PT", [P, BLK, BW])
        wqkv = PT[:, 0:3, :].rearrange("p a (b c) -> p (a b) c", c=CH)
        woutb = PT[:, 3, :].rearrange("p (b c) -> p b c", c=CH)
        hot, diag = PT[0:NBUCKET, 4, :], PT[0:HA, 5, :]
        NM = sb("NM", [P, 2, 32])
        DRING = 3
        D = sb("D", [P, DRING, BW], F32R)
        OS = sb("OS", [P, 2, BW])
        RC = sb("RC", [P, 2, 16])
        ON = sb("ON", [P, 2, 2, P])
        OT = sb("OT", [P, 2, 2, P])
        Y = sb("Y", [P, 2, CH])

        bank = [ctx.enter_context(nc.psum_tensor(f"bank{n}", [P, BW], F32)) for n in range(8)]
        S_BANK, Z_BANK, O_BANK, F_BANK, G_BANK = 0, 2, 4, 6, 7

        rows = nc.dram_tensor("bias_rows", (HA, NDIAG), F32, kind="Internal").ap()

        x_in = [sem(f"x_in{b}") for b in range(BATCH)]
        con_in, hot_in, rb_in, win_in, wouta_in = (sem(n) for n in ("con_in", "hot_in", "rb_in", "win_in", "wouta_in"))
        wqk_in, wqkv_in, woutb_in = sem("wqk_in"), sem("wqkv_in"), sem("woutb_in")
        rows_out, toep_in = sem("rows_out"), sem("toep_in")
        y_out = [sem(f"y_out{half}") for half in range(2)]
        fills, dve_fills = sem("fills"), sem("dve_fills")
        rounded = sem("rounded")
        spread_ready = sem("spread_ready")
        small_done, small_ready = sem("small_done"), sem("small_ready")
        diag_done, diag_ready = sem("diag_done"), sem("diag_ready")
        wqk_done, wqk_ready = sem("wqk_done"), sem("wqk_ready")
        wb_done, wb_ready = sem("wb_done"), sem("wb_ready")
        uh_ready, ul_ready = sem("uh_ready"), sem("ul_ready")
        part_ready, mean_done, mu_ready = sem("part_ready"), sem("mean_done"), sem("mu_ready")
        cent_ready, cent_pool, sq_ready = sem("cent_ready"), sem("cent_pool"), sem("sq_ready")
        part2_ready, var_done, sd_ready, rs_ready = sem("part2_ready"), sem("var_done"), sem("sd_ready"), sem("rs_ready")
        xn_dve, xn_pool = sem("xn_dve"), sem("xn_pool")
        xr_done, xr_ready = sem("xr_done"), sem("xr_ready")
        q_done, k_done, v_done = sem("q_done"), sem("k_done"), sem("v_done")
        qh_ready, kh_ready, q_ready, k_ready, v_ready = (sem(n) for n in ("qh_ready", "kh_ready", "q_ready", "k_ready", "v_ready"))
        vx_ready = sem("vx_ready")
        xt_done, gm_done, gv_done, xt_ready = sem("xt_done"), sem("gm_done"), sem("gv_done"), sem("xt_ready")
        agg_ready, mom_ready, gve_ready, grs_ready, gnb_ready = (sem(n) for n in ("agg_ready", "mom_ready", "gve_ready", "grs_ready", "gnb_ready"))
        stat_step, mom_step = sem("stat_step"), sem("mom_step")
        s_done, max_ready, d_ready = sem("s_done"), sem("max_ready"), sem("d_ready")
        km_ready, qk_ready = sem("km_ready"), sem("qk_ready")
        z_done, p_ready, pv_done, os_ready = sem("z_done"), sem("p_ready"), sem("pv_done"), sem("os_ready")
        t1_done, rc_ready, on_ready, t2_done, ot_ready, f_done = (sem(n) for n in ("t1_done", "rc_ready", "on_ready", "t2_done", "ot_ready", "f_done"))
        res_ready = sem("res_ready")

        block = ctx.enter_context(nc.Block())

        def is_a(i):
            return i < BATCH

        def halves(i):
            return i + 1 if is_a(i) else BATCH + 2 * (i - BATCH + 1)

        def grouped(t, b):
            return t[:, b].rearrange("p t (g c) -> p t g c", c=GC)

        def spread(t, b):
            return t[:, b].unsqueeze(1).unsqueeze(3).to_broadcast([P, TT, GRP, GC])

        def v_total(i):
            return i + 1 if is_a(i) else BATCH + 2 * (i - BATCH + 1)

        AHEAD = 2

        GROUPS = [(0, 1), (1, BATCH)]

        @block.sync
        def _(sp):
            sp.dma_start(X[:, 0], x[0].rearrange("(t p) c -> p t c", p=P)).then_inc(x_in[0], 16)
            sp.dma_start(rb[:], rel_bias).then_inc(rb_in, 16)
            sp.dma_start(hot, buckets).then_inc(hot_in, 16)
            for b in range(1, BATCH):
                sp.dma_start(X[:, b], x[b].rearrange("(t p) c -> p t c", p=P)).then_inc(x_in[b], 16)
            sp.wait_ge(diag_ready, 1)
            sp.dma_start(rows, diag).then_inc(rows_out, 16)
            sp.wait_ge(rows_out, 16)
            sp.dma_start(U, bass.AP(rows.tensor, 0, [[1, P], [NDIAG, HA], [1, TOEP]])).then_inc(toep_in, 16)
            sp.dma_start(wqkv, w_qkv.rearrange("(a p) c -> p a c", p=P)).then_inc(wqkv_in, 16)
            sp.dma_start(woutb, w_outb.rearrange("(a p) c -> p a c", p=P)).then_inc(woutb_in, 16)
            for i in range(BATCH, UNITS):
                for cp in range(2):
                    n = halves(i - 1) + cp + 1
                    sp.wait_ge(res_ready, n)
                    sp.dma_start(out[i - BATCH, cp * P:(cp + 1) * P, :], Y[:, cp]).then_inc(y_out[cp], 16)
            for half in range(2):
                sp.wait_ge(y_out[half], 16 * BATCH)

        @block.gpsimd
        def _(pool):
            pool.dma_start(con[:], consts).then_inc(con_in, 16)
            pool.dma_start(win[:], w_in).then_inc(win_in, 16)
            pool.dma_start(wouta[:], w_outa).then_inc(wouta_in, 16)
            pool.dma_start(wqk[:], w_qk.rearrange("(a p) c -> p a c", p=P)).then_inc(wqk_in, 16)
            pool.wait_ge(win_in, 16)
            nc.gpsimd.tensor_copy(wins[:], win[:].unsqueeze(2).to_broadcast([HA, HEIGHT, WIDTH])).then_inc(spread_ready, 1)
            pool.wait_ge(wouta_in, 16)
            nc.gpsimd.tensor_copy(woutas[:], wouta[:].unsqueeze(2).to_broadcast([HEIGHT, HA, HD])).then_inc(spread_ready, 1)
            nc.gpsimd.memset(VA[:, :, :, :, HD:], 1.0).then_inc(fills, 1)
            nc.gpsimd.memset(mhalf[:], -0.5).then_inc(fills, 1)
            pool.wait_ge(mu_ready, 1)
            for b in range(1, BATCH):
                nc.gpsimd.tensor_tensor(grouped(Xc, b), grouped(X, b), spread(Mu, b), op=ALU.subtract).then_inc(cent_pool, 1)
            pool.wait_ge(rs_ready, 2)
            for b in range(1, BATCH):
                nc.gpsimd.tensor_tensor(grouped(Xn, b), grouped(Xc, b), spread(Rs, b), op=ALU.mult).then_inc(xn_pool, 1)
                if b == 1:
                    for h in range(HA):
                        pool.wait_ge(uh_ready, h + 1)
                        nc.gpsimd.tensor_tensor(Ul[:, h], U[:, h], Uh[:, h].bitcast(F32), op=ALU.subtract).then_inc(ul_ready, 1)

            for n in range(3):
                pool.wait_ge(ul_ready, HA)
                pool.wait_ge(fills, 2 + 3 * n)
                nc.gpsimd.memset(VB[:, n, 1:, :, HD:], 1.0).then_inc(fills, 1)
                pool.wait_ge(fills, 3 + 3 * n)
                nc.gpsimd.memset(VB[0:CHUNK, n, 0, :, HD:], 1.0).then_inc(fills, 1)
                pool.wait_ge(fills, 4 + 3 * n)
                nc.gpsimd.memset(VB[CHUNK:, n, 0], 0.0).then_inc(fills, 1)

            def head_queries(i, u):
                b, idx = i - BATCH, (i - BATCH) * BLK + u
                cp, g, quad = u // 4, u // 2 % 2, u % 2
                if u == 0:
                    pool.wait_ge(qh_ready, i + 1)
                if idx >= QRING:
                    pool.wait_ge(z_done, i * BLK + u - QRING + 1)
                nc.gpsimd.tensor_tensor(Qk[:, idx % QRING, :].rearrange("p (h q) -> p h q", h=4),
                                        Qn[:, b % 3, g, cp * P:(cp + 1) * P].unsqueeze(1).to_broadcast([P, 4, P]),
                                        con[:, C_HEAD + 4 * quad:C_HEAD + 4 * quad + 4].unsqueeze(2).to_broadcast([P, 4, P]),
                                        op=ALU.mult).then_inc(qk_ready, 1)

            def scale_b(b):
                if b:
                    pool.wait_ge(xt_ready, b)
                else:
                    pool.wait_ge(fills, 11)
                pool.wait_ge(gve_ready, b + 1)
                nc.gpsimd.tensor_tensor(grs[:], gve[:], mhalf[:], op=ALU.pow).then_inc(grs_ready, 1)

            def window_values(b):
                n = b % 3
                pool.wait_ge(v_ready, v_total(BATCH + b))
                pool.wait_ge(grs_ready, b + 1)
                if b:
                    pool.wait_ge(qk_ready, (b - 1) * BLK + AHEAD + 2)
                nc.gpsimd.tensor_copy(VB[0:CHUNK, n, 0, :, 0:HD], VB[0:CHUNK, n, 1, :, 0:HD]).then_inc(vx_ready, 1)
                pool.wait_ge(vx_ready, 3 * b + 1)
                nc.gpsimd.tensor_copy(VB[0:CHUNK, n, 2, :, 0:HD], VB[0:CHUNK, n, 3, :, 0:HD]).then_inc(vx_ready, 1)
                pool.wait_ge(vx_ready, 3 * b + 2)
                nc.gpsimd.tensor_copy(VB[CHUNK:, n, 2, :, 0:HD], VB[CHUNK:, n, 1, :, 0:HD]).then_inc(vx_ready, 1)
                pool.wait_ge(vx_ready, 3 * b + 3)

            for i in range(BATCH - 1, UNITS + 1):
                for u in range(BLK):
                    ahead = (i - 1) * BLK + u + AHEAD
                    if BATCH * BLK <= ahead < UNITS * BLK:
                        head_queries(ahead // BLK, ahead % BLK)
                    if BATCH <= i + 1 < UNITS and u == 3:
                        scale_b(i + 1 - BATCH)
                    if BATCH <= i < UNITS and u == 1:
                        window_values(i - BATCH)

        @block.tensor
        def _(pe):
            ident = con[:, C_ID:C_ID + P]

            pe.wait_ge(con_in, 16)
            pe.wait_ge(spread_ready, 2)
            small = bank[Z_BANK]
            for t in range(TT):
                lhs = wins[:, t * 8:(t + 1) * 8, :].rearrange("h c f -> h (c f)")
                nc.tensor.matmul(small[:, t * HA:(t + 1) * HA], lhs, con[0:HA, C_ID:C_ID + HA], start=True, stop=True)
            lhs = woutas[:].rearrange("c h f -> c (h f)")
            nc.tensor.matmul(small[:, 64:64 + HEIGHT], lhs, con[0:HEIGHT, C_ID:C_ID + HEIGHT], start=True, stop=True).then_inc(small_done, 1)
            pe.wait_ge(rb_in, 16)
            pe.wait_ge(hot_in, 16)
            nc.tensor.matmul(bank[Z_BANK + 1][0:HA, :], rb[:], hot, start=True, stop=True).then_inc(diag_done, 1)
            pe.wait_ge(wqk_in, 16)
            for a in range(2):
                last = nc.tensor.transpose(bank[O_BANK][:, a * P:(a + 1) * P], wqk[:, a, :], ident)
            last.then_inc(wqk_done, 1)

            def moments(g, which, ready, done):
                b0, b1 = GROUPS[g]
                pe.wait_ge(ready, g + 1)
                if g:
                    pe.wait_ge(rs_ready, 1)
                col = 256 * which
                for t in range(TT):
                    last = nc.tensor.matmul(bank[O_BANK + 1][:, col:col + (b1 - b0) * GRP], avg[:],
                                            Part[:, which, b0:b1, t, :], start=(t == 0), stop=(t == TT - 1))
                last.then_inc(done, 1)

            def wait_bank_f(i):
                if i > 0:
                    pe.wait_ge(v_ready, v_total(i - 1))

            def project_a(i, step):
                f = bank[F_BANK]
                if step == 0:
                    if i == 0:
                        pe.wait_ge(xn_dve, 1)
                        pe.wait_ge(small_ready, 2)
                    else:
                        pe.wait_ge(xn_pool, i)
                    wait_bank_f(i)
                    for t in range(TT):
                        last = nc.tensor.matmul(f[:, 0:CH], WinK[:, t, :], Xn[:, i, t, :], start=(t == 0), stop=(t == TT - 1))
                    last.then_inc(xr_done, 1)
                if step == 1:
                    if i == 0:
                        pe.wait_ge(wqk_ready, 2)
                    pe.wait_ge(xr_ready, i + 1)
                    for t in range(2):
                        last = nc.tensor.matmul(f[:, t * CH:(t + 1) * CH], WQ[:, t, :], XR[:], start=True, stop=True)
                    last.then_inc(q_done, 1)
                if step == 2:
                    pe.wait_ge(q_ready, i + 1)
                    for t in range(2):
                        last = nc.tensor.matmul(f[:, t * CH:(t + 1) * CH], WK[:, t, :], XR[:], start=True, stop=True)
                    last.then_inc(k_done, 1)
                if step == 3:
                    pe.wait_ge(k_ready, i + 1)
                    for m in range(2):
                        for t in range(TT):
                            last = nc.tensor.matmul(f[:, m * P:(m + 1) * P], Xn[:, i, t, m * P:(m + 1) * P], WinK[:, t, :],
                                                    start=(t == 0), stop=(t == TT - 1))
                    last.then_inc(v_done, 1)

            def project_b(i, step):
                b = i - BATCH
                f, m = bank[F_BANK], bank[G_BANK]
                if step == 0:
                    pe.wait_ge(res_ready, b + 1)
                    wait_bank_f(i)
                    for k in range(CT):
                        for t in range(TT):
                            last = nc.tensor.transpose(f[:, k * TOK + t * P:k * TOK + (t + 1) * P],
                                                       X1[:, b, t, k * P:(k + 1) * P], ident)
                    last.then_inc(xt_done, 1)
                if step == 1:
                    pe.wait_ge(agg_ready, b + 1)
                    if b:
                        pe.wait_ge(gve_ready, b)
                    else:
                        pe.wait_ge(wb_ready, 4)
                    nc.tensor.matmul(m[:, 0:CT], con[:, C_GRP:C_GRP + P], agg[:, :, 0], start=True, stop=True).then_inc(gm_done, 1)
                if step == 2:
                    pe.wait_ge(mom_ready, b + 1)
                    nc.tensor.matmul(m[:, 4:4 + CT], con[:, C_GRP:C_GRP + P], mom[:], start=True, stop=True).then_inc(gv_done, 1)
                if step in (3, 4):
                    if step == 3:
                        pe.wait_ge(xt_ready, b + 1)
                    else:
                        pe.wait_ge(q_ready, i + 1)
                    for g in range(2):
                        for k in range(CT):
                            col = (step - 3) * CH + g * P
                            last = nc.tensor.matmul(f[:, g * TOK:(g + 1) * TOK], WT[:, k, col:col + P], XT[:, k, :],
                                                    start=(k == 0), stop=(k == CT - 1))
                    last.then_inc(q_done if step == 3 else k_done, 1)
                if step == 5:
                    pe.wait_ge(kh_ready, i + 1)
                    for t in range(TT):
                        for k in range(CT):
                            last = nc.tensor.matmul(f[:, t * CH:(t + 1) * CH], XT[:, k, t * P:(t + 1) * P], WT[:, k, 2 * CH:],
                                                    start=(k == 0), stop=(k == CT - 1))
                    last.then_inc(v_done, 1)

            def scores_a(i, u):
                s = bank[S_BANK + u % 2]
                n, q, r = i % 3, u // 4, 32 * (u % 4)
                if i == 0:
                    pe.wait_ge(uh_ready, u + 1)
                for nt in range(2):
                    for mt in range(2):
                        col = (nt + 1 - mt) * P
                        nc.tensor.matmul(s[:, nt * CH + mt * P:nt * CH + (mt + 1) * P], Uh[:, u, col:col + P], revr[:],
                                         start=(nt + mt == 0), stop=False, skip_group_check=True)
                for nt in range(2):
                    last = nc.tensor.matmul(s[:, nt * CH:(nt + 1) * CH], Qst[r:r + 32, n, q, nt * P:(nt + 1) * P],
                                            KH[r:r + 32, n, q, :], start=False, stop=(nt == 1), skip_group_check=True)
                return last

            def scores_b(i, u):
                s = bank[S_BANK + u % 2]
                b = i - BATCH
                cp, g, quad = u // 4, u // 2 % 2, u % 2
                pe.wait_ge(km_ready, 4 * b + u % 4 + 1)
                for c2 in range(2):
                    c = 2 * cp + c2
                    keys = Km[:, g, 4 * quad:4 * quad + 4, :]
                    if c == 0:
                        rhs = keys[:, :, 0:CHUNK].unsqueeze(2).to_broadcast([P, 4, 2, CHUNK])
                    else:
                        rhs = keys[:, :, (c - 1) * CHUNK:(c + 1) * CHUNK]
                    pair = Qs[:, b % 2, g, cp].rearrange("p a q -> p (a q)")
                    last = nc.tensor.matmul(s[:], pair[:, c2 * CHUNK:(c2 + 2) * CHUNK], rhs, start=(c2 == 0), stop=(c2 == 1))
                return last

            def shifted_a(i, u):
                z = bank[Z_BANK + u % 2]
                n, q, r = i % 3, u // 4, 32 * (u % 4)
                if i == 0:
                    pe.wait_ge(ul_ready, u + 1)
                for table in (Uh, Ul):
                    strip = table[:, u, :]
                    strip = bass.AP(strip.tensor, strip.offset, [strip.ap[0], [P, 2], [1, CH]])
                    nc.tensor.matmul(z[:], revr[:], strip, start=(table is Uh), stop=False, skip_group_check=True)
                zs = z[:].rearrange("p (s n) -> p s n", s=2)
                nc.tensor.matmul(z[:], minus[:], D[:, (i * BLK + u) % DRING, 0:CH].unsqueeze(1).to_broadcast([P, 2, CH]),
                                 start=False, stop=False, skip_group_check=True)
                for s in range(2):
                    mt = 1 - s
                    for keys in (KH, KL):
                        last = nc.tensor.matmul(zs[:, s, :], keys[r:r + 32, n, q, mt * P:(mt + 1) * P], Qst[r:r + 32, n, q, :],
                                                start=False, stop=(s == 1 and keys is KL), skip_group_check=True)
                return last

            def shifted_b(i, u):
                z = bank[Z_BANK + u % 2]
                b = i - BATCH
                cp, g = u // 4, u // 2 % 2
                nc.tensor.matmul(z[:], minus[:], D[:, (i * BLK + u) % DRING, :], start=True, stop=False, skip_group_check=True)
                pe.wait_ge(qk_ready, b * BLK + u + 1)
                heads = Qk[:, (b * BLK + u) % QRING, :].rearrange("p (h c q) -> p h c q", h=4, c=2)
                zs = z[:].rearrange("p (h c q) -> p h c q", h=4, c=2)
                for c2 in range(2):
                    w = WINDOW[2 * cp + c2] * CHUNK
                    last = nc.tensor.matmul(zs[:, :, c2, :], Kf[:, b % 3, g, w:w + 2 * CHUNK], heads[:, :, c2, :],
                                            start=False, stop=(c2 == 1), skip_group_check=True)
                return last

            def scores(i, u):
                idx = i * BLK + u
                if u == 0:
                    pe.wait_ge(q_ready, i + 1)
                    if is_a(i):
                        pe.wait_ge(k_ready, i + 1)
                if idx >= 2:
                    pe.wait_ge(max_ready, idx - 1)
                (scores_a if is_a(i) else scores_b)(i, u).then_inc(s_done, 1)

            def shifted(i, u):
                idx = i * BLK + u
                pe.wait_ge(d_ready, idx + 1)
                if not is_a(i) and u == 0:
                    pe.wait_ge(kh_ready, i + 1)
                if idx >= 2:
                    pe.wait_ge(p_ready, idx - 1)
                (shifted_a if is_a(i) else shifted_b)(i, u).then_inc(z_done, 1)

            def values(i, half):
                o = bank[O_BANK + half]
                pe.wait_ge(p_ready, i * BLK + 4 * (half + 1))
                if half == 0:
                    if is_a(i):
                        pe.wait_ge(v_ready, v_total(i))
                        if i == 0:
                            pe.wait_ge(fills, 1)
                    else:
                        pe.wait_ge(vx_ready, 3 * (i - BATCH + 1))
                    if i == 0:
                        pe.wait_ge(wb_ready, 4)
                if i > 0:
                    if half == 0 or not is_a(i - 1):
                        pe.wait_ge(res_ready, halves(i - 1) - (0 if is_a(i - 1) else 1 - half))
                    else:
                        pe.wait_ge(ot_ready, halves(i - 1))
                if is_a(i):
                    for mt in range(2):
                        for hh in range(4):
                            last = nc.tensor.matmul(o[32 * hh:32 * hh + 32, 0:CH], VA[:, i % 3, mt, 4 * half + hh, :],
                                                    PT[:, 4 * half + hh, (1 - mt) * CH:(2 - mt) * CH],
                                                    start=(mt == 0), stop=(mt == 1))
                else:
                    for j in range(4):
                        for c2 in range(2):
                            for hh in range(4):
                                h = 4 * j + hh
                                col = j * P + c2 * CHUNK
                                last = nc.tensor.matmul(o[32 * hh:32 * hh + 32, col:col + CHUNK],
                                                        VB[:, (i - BATCH) % 3, 2 * half + c2, h, :],
                                                        PT[:, 4 * half + j, hh * P + c2 * CHUNK:hh * P + (c2 + 1) * CHUNK],
                                                        start=True, stop=True)
                last.then_inc(pv_done, 1)

            def finish(i, half, step):
                n = halves(i - 1) + (half if not is_a(i) else 0) if i else 0
                o = bank[O_BANK + half]
                if step == 0:
                    if is_a(i):
                        pe.wait_ge(os_ready, 2 * (i + 1))
                        for nt in range(2):
                            for q in range(2):
                                col = (2 * nt + q) * P
                                last = nc.tensor.transpose(o[:, col:col + P], OS[:, q, nt * P:(nt + 1) * P], ident)
                    else:
                        pe.wait_ge(os_ready, 2 * i + half + 1)
                        for j in range(4):
                            last = nc.tensor.transpose(o[:, j * P:(j + 1) * P], OS[:, half, j * P:(j + 1) * P], ident)
                    last.then_inc(t1_done, 1)
                if step == 1:
                    pe.wait_ge(on_ready, n + 1)
                    t2 = bank[O_BANK + 1] if is_a(i) else o
                    for k in range(2):
                        src = ON[:, k, 0, :] if is_a(i) else ON[:, half, k, :]
                        last = nc.tensor.transpose(t2[:, k * P:(k + 1) * P], src, ident)
                    last.then_inc(t2_done, 1)
                if step == 2:
                    pe.wait_ge(ot_ready, n + 1)
                    if is_a(i):
                        for t in range(TT):
                            last = nc.tensor.matmul(o[:, t * CH:(t + 1) * CH], WoutK[:, t, :],
                                                    OT[:, 0, :, :].rearrange("p a b -> p (a b)"), start=True, stop=True)
                    else:
                        for g in range(2):
                            last = nc.tensor.matmul(o[:, 0:CH], OT[:, half, g, :], WoT[:, g, :], start=(g == 0), stop=(g == 1))
                    last.then_inc(f_done, 1)

            def weights_b():
                pe.wait_ge(wqkv_in, 16)
                pe.wait_ge(woutb_in, 16)
                pe.wait_ge(small_ready, 2)
                pe.wait_ge(diag_ready, 1)
                pe.wait_ge(wqk_ready, 2)
                pe.wait_ge(rs_ready, 2)
                for n in range(4):
                    for m in range(4):
                        if n < 3:
                            src = wqkv[:, 2 * n + m % 2, (m // 2) * P:(m // 2 + 1) * P]
                        else:
                            src = woutb[:, m % 2, (m // 2) * P:(m // 2 + 1) * P]
                        last = nc.tensor.transpose(bank[Z_BANK + n][:, m * P:(m + 1) * P], src, ident)
                    last.then_inc(wb_done, 1)

            pe.wait_ge(dve_fills, 1)
            moments(0, 0, part_ready, mean_done)
            moments(0, 1, part2_ready, var_done)
            for step in range(4):
                project_a(0, step)
            moments(1, 0, part_ready, mean_done)
            moments(1, 1, part2_ready, var_done)
            weights_b()
            pe.wait_ge(rounded, 2)
            for i in range(UNITS + 2):
                for u in range(BLK):
                    if i < UNITS:
                        scores(i, u)
                    if 0 < i <= UNITS:
                        shifted(i - 1, u)
                    if 1 < i <= UNITS + 1:
                        if u == 0:
                            values(i - 2, 1)
                        if not is_a(i - 2):
                            if u == 0:
                                finish(i - 2, 0, 2)
                            if 1 <= u <= 3:
                                finish(i - 2, 1, u - 1)
                        elif 1 <= u <= 3:
                            finish(i - 2, 0, u - 1)
                    if i + 1 < BATCH and u in (0, 2, 4, 6):
                        project_a(i + 1, u // 2)
                    if BATCH <= i + 1 < UNITS and u in (0, 1, 2, 4, 5, 6):
                        project_b(i + 1, (0, 1, 2, 4, 5, 6).index(u))
                    if 0 < i <= UNITS:
                        if u == 5:
                            values(i - 1, 0)
                        if not is_a(i - 1) and u in (6, 7):
                            finish(i - 1, 0, u - 6)

        @block.vector
        def _(dve):
            V = nc.vector
            V.memset(avg[:], 1.0 / (TOK * GC)).then_inc(dve_fills, 1)
            V.memset(eps[:], EPS).then_inc(dve_fills, 1)

            def part_sums(g, src, which, done):
                b0, b1 = GROUPS[g]
                V.tensor_reduce(Part[:, which, b0:b1].rearrange("p b t g -> p (b t g)"),
                                src[:, b0:b1].rearrange("p b t (g c) -> p (b t g) c", c=GC), AX.X, ALU.add).then_inc(done, 1)

            def norm_x(g, step):
                b0, b1 = GROUPS[g]
                m = bank[O_BANK + 1]
                if step == 0:
                    for b in range(b0, b1):
                        dve.wait_ge(x_in[b], 16)
                    part_sums(g, X, 0, part_ready)
                if step == 1:
                    dve.wait_ge(mean_done, g + 1)
                    if g == 0:
                        mean = m[:, 0:GRP].unsqueeze(1).unsqueeze(3).to_broadcast([P, TT, GRP, GC])
                        V.tensor_tensor(grouped(Xc, 0), grouped(X, 0), mean, op=ALU.subtract).then_inc(cent_ready, 1)
                    else:
                        V.tensor_copy(Mu[:, b0:b1].rearrange("p b g -> p (b g)"), m[:, 0:(b1 - b0) * GRP]).then_inc(mu_ready, 1)
                if step == 2:
                    dve.wait_ge(sq_ready, b1)
                    part_sums(g, Sq, 1, part2_ready)
                if step == 3:
                    dve.wait_ge(sd_ready, g + 1)
                    V.reciprocal(Rs[:, b0:b1], Sd[:, b0:b1]).then_inc(rs_ready, 1)
                    if g == 0:
                        dve.wait_ge(rs_ready, 1)
                        V.tensor_tensor(grouped(Xn, 0), grouped(Xc, 0), spread(Rs, 0), op=ALU.mult).then_inc(xn_dve, 1)

            def small_weights():
                dve.wait_ge(con_in, 16)
                dve.wait_ge(small_done, 1)
                sub = con[:, C_SUB:C_SUB + HD]
                small = bank[Z_BANK]
                V.tensor_tensor(WinK[:].rearrange("p t (h f) -> p (t h) f", f=HD),
                                small[:, 0:TT * HA].unsqueeze(2).to_broadcast([P, TT * HA, HD]),
                                sub.unsqueeze(1).to_broadcast([P, TT * HA, HD]), op=ALU.mult).then_inc(small_ready, 1)
                V.tensor_tensor(WoutK[:].rearrange("p t (c f) -> p (t c) f", f=WIDTH),
                                small[:, 64:64 + HEIGHT].unsqueeze(2).to_broadcast([P, HEIGHT, WIDTH]),
                                sub.unsqueeze(1).to_broadcast([P, HEIGHT, WIDTH]), op=ALU.mult).then_inc(small_ready, 1)
                dve.wait_ge(wqk_done, 1)
                for k, w in enumerate((WQ, WK)):
                    src = bank[O_BANK][:, 0:2 * P].rearrange("p (h k d) -> p h k d", k=2, d=HD)[:, :, k, :]
                    V.tensor_copy(w[:].rearrange("p t (h r d) -> p (t h) r d", r=2, d=HD),
                                  src.unsqueeze(2).to_broadcast([P, HA, 2, HD])).then_inc(wqk_ready, 1)

            def queries_keys(i, which):
                f = bank[F_BANK]
                if is_a(i):
                    if which == 0:
                        if i >= 3:
                            dve.wait_ge(z_done, BLK * (i - 2))
                        dve.wait_ge(qh_ready, i + 1)
                        V.scalar_tensor_tensor(Qst[:, i % 3].rearrange("p t n -> p (t n)"),
                                               QH[:].rearrange("p t n -> p (t n)").bitcast(F32), con[:, C_LOW:C_LOW + 1], f[:],
                                               ALU.mult, ALU.add).then_inc(q_ready, 1)
                    else:
                        dve.wait_ge(kh_ready, i + 1)
                        V.tensor_tensor(KL[:, i % 3].rearrange("p t n -> p (t n)"), f[:],
                                        KH[:, i % 3].rearrange("p t n -> p (t n)").bitcast(F32), op=ALU.subtract).then_inc(k_ready, 1)
                else:
                    b = i - BATCH
                    if which == 0:
                        dve.wait_ge(qh_ready, i + 1)
                        if b >= 2:
                            dve.wait_ge(s_done, BLK * (i - 1))
                        V.tensor_copy(Qs[:, b % 2, :, :, 0:3:2, :], Qn[:, b % 3].rearrange("p g (a c q) -> p g a c q", a=2, c=2)).then_inc(q_ready, 1)

            def head_keys(i, part):
                b = i - BATCH
                g, quad = part // 2, part % 2
                dve.wait_ge(kh_ready, i + 1)
                if b:
                    dve.wait_ge(s_done, BLK * (i - 1) + 4 + part + 1)
                for h in range(4 * quad, 4 * quad + 4):
                    last = V.tensor_scalar(Km[:, g, h, :], Kf[:, b % 3, g, CHUNK:CHUNK + TOK],
                                           con[:, C_HEAD + h:C_HEAD + h + 1], None, ALU.mult)
                last.then_inc(km_ready, 1)

            def value_rows(i):
                f = bank[F_BANK]
                dve.wait_ge(v_done, i + 1)
                if is_a(i):
                    if i >= 3:
                        dve.wait_ge(pv_done, 2 * (i - 2))
                    V.tensor_copy(VA[:, i % 3, :, :, 0:HD], f[:, 0:2 * P].rearrange("p (m h d) -> p m h d", m=2, d=HD)).then_inc(v_ready, 1)
                else:
                    b = i - BATCH
                    if b == 0:
                        dve.wait_ge(fills, 11)
                    if b >= 3:
                        dve.wait_ge(pv_done, 2 * (i - 2))
                        dve.wait_ge(vx_ready, 3 * (b - 2))
                    for t in range(TT):
                        V.tensor_copy(VB[:, b % 3, 2 * t + 1, :, 0:HD],
                                      f[:, t * CH:(t + 1) * CH].rearrange("p (h d) -> p h d", d=HD)).then_inc(v_ready, 1)

            def norm_b(b, step):
                m = bank[G_BANK]
                c0 = 4 * b
                if step == 0:
                    dve.wait_ge(xt_done, b + 1)
                    for k in range(CT):
                        V.bn_stats(bst[:, k, :], bank[F_BANK][:, k * TOK:(k + 1) * TOK]).then_inc(stat_step, 1)
                    dve.wait_ge(stat_step, c0 + 2)
                    if b:
                        dve.wait_ge(gm_done, b)
                    for k in range(CT):
                        last = V.bn_aggr(agg[:, k, :], bst[:, k, :])
                    last.then_inc(agg_ready, 1)
                if step == 1:
                    dve.wait_ge(gm_done, b + 1)
                    V.tensor_copy(gm[:], m[:, 0:CT]).then_inc(stat_step, 1)
                    dve.wait_ge(agg_ready, b + 1)
                    dve.wait_ge(stat_step, c0 + 3)
                    V.tensor_tensor(dev[:], agg[:, :, 0], gm[:], op=ALU.subtract).then_inc(stat_step, 1)
                    dve.wait_ge(stat_step, c0 + 4)
                    V.tensor_tensor(dsq[:], dev[:], dev[:], op=ALU.mult).then_inc(mom_step, 1)
                    dve.wait_ge(mom_step, b + 1)
                    V.tensor_tensor(mom[:], dsq[:], agg[:, :, 1], op=ALU.add).then_inc(mom_ready, 1)
                if step == 2:
                    dve.wait_ge(gv_done, b + 1)
                    V.tensor_scalar(gve[:], m[:, 4:4 + CT], EPS, None, ALU.add).then_inc(gve_ready, 1)
                if step == 3:
                    dve.wait_ge(grs_ready, b + 1)
                    V.scalar_tensor_tensor(gnb[:], gm[:], -1.0, grs[:], ALU.mult, ALU.mult).then_inc(gnb_ready, 1)

            def block_max(i, u):
                dve.wait_ge(s_done, i * BLK + u + 1)
                s = bank[S_BANK + u % 2]
                if i >= 2:
                    dve.wait_ge(d_ready, (i - 2) * BLK + u + 1)
                if is_a(i):
                    V.tensor_reduce(NM[:, i % 2, 2 * u:2 * u + 2], s[:].rearrange("p (n m) -> p n m", n=2), AX.X, ALU.max).then_inc(max_ready, 1)
                else:
                    V.tensor_reduce(NM[:, i % 2, 4 * u:4 * u + 4], s[:].rearrange("p (h m) -> p h m", h=4), AX.X, ALU.max).then_inc(max_ready, 1)

            def diagonal(i, u):
                idx = i * BLK + u
                n = 2 if is_a(i) else 4
                dve.wait_ge(max_ready, idx + 1)
                if idx >= DRING:
                    dve.wait_ge(z_done, idx - DRING + 1)
                V.tensor_tensor(D[:, idx % DRING, 0:n * P].rearrange("p (h q) -> p h q", h=n),
                                con[:, C_ID:C_ID + P].unsqueeze(1).to_broadcast([P, n, P]),
                                NM[:, i % 2, n * u:n * u + n].unsqueeze(2).to_broadcast([P, n, P]), op=ALU.mult).then_inc(d_ready, 1)

            def divide(i, half):
                n = (halves(i - 1) if i else 0) + (0 if is_a(i) else half)
                o = bank[O_BANK + half]
                dve.wait_ge(t1_done, n + 1)
                V.reciprocal(RC[:, half, :], o[:].rearrange("p (a z) -> p a z", z=32)[:, :, HD]).then_inc(rc_ready, 1)
                dve.wait_ge(rc_ready, n + 1)
                if is_a(i):
                    V.tensor_tensor(ON[:, :, 0, :].rearrange("p n (h d) -> p n h d", d=HD),
                                    o[:].rearrange("p (n h z) -> p n h z", n=2, z=32)[:, :, :, 0:HD],
                                    RC[:, half, :].rearrange("p (n h) -> p n h", n=2).unsqueeze(3).to_broadcast([P, 2, HA, HD]),
                                    op=ALU.mult).then_inc(on_ready, 1)
                else:
                    V.tensor_tensor(ON[:, half].rearrange("p g (h d) -> p (g h) d", d=HD),
                                    o[:].rearrange("p (h z) -> p h z", z=32)[:, :, 0:HD],
                                    RC[:, half, :].unsqueeze(2).to_broadcast([P, HB, HD]), op=ALU.mult).then_inc(on_ready, 1)

            def residual(i, half):
                n = (halves(i - 1) if i else 0) + (0 if is_a(i) else half)
                o = bank[O_BANK + half]
                dve.wait_ge(f_done, n + 1)
                if is_a(i):
                    V.tensor_tensor(X1[:, i].rearrange("p t c -> p (t c)"), o[:], X[:, i].rearrange("p t c -> p (t c)"),
                                    op=ALU.add).then_inc(res_ready, 1)
                else:
                    b = i - BATCH
                    if b:
                        dve.wait_ge(y_out[half], 16 * b)
                    V.tensor_tensor(Y[:, half], o[:, 0:CH], X1[:, b, half, :], op=ALU.add).then_inc(res_ready, 1)

            norm_x(0, 0)
            norm_x(1, 0)
            small_weights()
            dve.wait_ge(diag_done, 1)
            V.tensor_copy(diag, bank[Z_BANK + 1][0:HA, :]).then_inc(diag_ready, 1)
            norm_x(0, 1)
            norm_x(0, 2)
            norm_x(0, 3)
            V.tensor_copy(revr[:], con[:, C_REV:C_REV + P]).then_inc(rounded, 1)
            for n in range(2):
                V.tensor_scalar(Qs[:, n, :, :, 1, :], con[:, C_ID:C_ID + CHUNK].unsqueeze(1).unsqueeze(1).to_broadcast([P, 2, 2, CHUNK]),
                                0.0, None, ALU.mult)
            V.tensor_scalar(minus[:], con[:, C_ID:C_ID + P], 0.0, -1.0, ALU.mult, ALU.add).then_inc(rounded, 1)
            queries_keys(0, 0)
            queries_keys(0, 1)
            value_rows(0)
            norm_x(1, 1)
            norm_x(1, 2)
            norm_x(1, 3)
            for i in range(UNITS + 2):
                for u in range(BLK):
                    ahead = (i - 1) * BLK + u + AHEAD
                    if 0 <= ahead < UNITS * BLK:
                        diagonal(ahead // BLK, ahead % BLK)
                    if i < UNITS:
                        block_max(i, u)
                    if 1 < i <= UNITS + 1:
                        if not is_a(i - 2):
                            if u == 0:
                                residual(i - 2, 0)
                            if u == 1:
                                divide(i - 2, 1)
                            if u == 3:
                                residual(i - 2, 1)
                        else:
                            if u == 1:
                                divide(i - 2, 0)
                            if u == 3:
                                residual(i - 2, 0)
                    if i + 1 < BATCH:
                        if u == 2:
                            queries_keys(i + 1, 0)
                        if u == 4:
                            queries_keys(i + 1, 1)
                        if u == 6:
                            value_rows(i + 1)
                    if BATCH <= i + 1 < UNITS:
                        if u in (0, 1, 2, 3):
                            norm_b(i + 1 - BATCH, u)
                        if u == 4:
                            queries_keys(i + 1, 0)
                        if u == 6:
                            value_rows(i + 1)
                            head_keys(i + 1, 0)
                            head_keys(i + 1, 1)
                        if u == 7:
                            head_keys(i + 1, 2)
                            head_keys(i + 1, 3)
                    if 0 < i <= UNITS and not is_a(i - 1) and u == 6:
                        divide(i - 1, 0)

        @block.scalar
        def _(act):
            A = nc.scalar
            act.wait_ge(dve_fills, 2)

            def squares(g):
                b0, b1 = GROUPS[g]
                for b in range(b0, b1):
                    if g == 0:
                        act.wait_ge(cent_ready, 1)
                    else:
                        act.wait_ge(cent_pool, b)
                    A.activation(Sq[:, b], Xc[:, b], ACT.Square).then_inc(sq_ready, 1)

            def deviation(g):
                b0, b1 = GROUPS[g]
                act.wait_ge(var_done, g + 1)
                A.activation(Sd[:, b0:b1].rearrange("p b g -> p (b g)"), bank[O_BANK + 1][:, 256:256 + (b1 - b0) * GRP],
                             ACT.Sqrt, bias=eps[:]).then_inc(sd_ready, 1)

            def weights_b(n):
                act.wait_ge(wb_done, n + 1)
                src = bank[Z_BANK + n][:].rearrange("p (k r) -> p k r", k=2)
                dst = WT[:, :, n * CH:(n + 1) * CH] if n < 3 else WoT[:]
                A.activation(dst, src, ACT.Copy).then_inc(wb_ready, 1)

            def projected(i, which):
                f = bank[F_BANK]
                if is_a(i):
                    if which == 0:
                        act.wait_ge(xr_done, i + 1)
                        if i:
                            act.wait_ge(k_done, i)
                        A.activation(XR[:], f[:, 0:CH], ACT.Copy).then_inc(xr_ready, 1)
                    if which == 1:
                        act.wait_ge(q_done, i + 1)
                        if i:
                            act.wait_ge(q_ready, i)
                        A.activation(QH[:].rearrange("p t n -> p (t n)"), f[:], ACT.Copy).then_inc(qh_ready, 1)
                    if which == 2:
                        act.wait_ge(k_done, i + 1)
                        if i >= 3:
                            act.wait_ge(z_done, BLK * (i - 2))
                        A.activation(KH[:, i % 3].rearrange("p t n -> p (t n)"), f[:], ACT.Copy).then_inc(kh_ready, 1)
                else:
                    b = i - BATCH
                    if which == 0:
                        act.wait_ge(gnb_ready, b + 1)
                        for k in range(CT):
                            last = A.activation(XT[:, k, :], f[:, k * TOK:(k + 1) * TOK], ACT.Identity,
                                                bias=gnb[:, k:k + 1], scale=grs[:, k:k + 1])
                        last.then_inc(xt_ready, 1)
                    if which == 1:
                        act.wait_ge(q_done, i + 1)
                        if b >= 3:
                            act.wait_ge(qk_ready, BLK * (b - 2))
                        A.activation(Qn[:, b % 3].rearrange("p g n -> p (g n)"), f[:], ACT.Copy).then_inc(qh_ready, 1)
                    if which == 2:
                        act.wait_ge(k_done, i + 1)
                        if b >= 3:
                            act.wait_ge(z_done, BLK * (i - 2))
                        src = f[:].rearrange("p (g n) -> p g n", g=2)
                        for slot, c, m in ((0, 0, 1), (1, 0, 4), (5, 2, 1), (6, 1, 1)):
                            last = A.activation(Kf[:, b % 3, :, slot * CHUNK:(slot + m) * CHUNK],
                                                src[:, :, c * CHUNK:(c + m) * CHUNK], ACT.Copy)
                        last.then_inc(kh_ready, 1)

            def probabilities(i, u):
                act.wait_ge(z_done, i * BLK + u + 1)
                if i >= 1 and u % 4 == 0:
                    act.wait_ge(pv_done, 2 * (i - 1) + u // 4 + 1)
                A.activation(PT[:, u, :], bank[Z_BANK + u % 2][:], ACT.Exp, scale=SCALE).then_inc(p_ready, 1)

            def unnormalised(i, half):
                act.wait_ge(pv_done, 2 * i + half + 1)
                if i:
                    act.wait_ge(t1_done, halves(i - 1) - (0 if is_a(i - 1) else 1 - half))
                w = CH if is_a(i) else BW
                A.activation(OS[:, half, 0:w], bank[O_BANK + half][:, 0:w], ACT.Copy).then_inc(os_ready, 1)

            def normalised(i, half):
                n = (halves(i - 1) if i else 0) + (0 if is_a(i) else half)
                t2 = bank[O_BANK + 1] if is_a(i) else bank[O_BANK + half]
                act.wait_ge(t2_done, n + 1)
                if i:
                    act.wait_ge(f_done, halves(i - 1) - (0 if is_a(i - 1) else 1 - half))
                A.activation(OT[:, 0 if is_a(i) else half].rearrange("p a b -> p (a b)"), t2[:, 0:2 * P], ACT.Copy).then_inc(ot_ready, 1)

            squares(0)
            deviation(0)
            for which in range(3):
                projected(0, which)
            squares(1)
            deviation(1)
            act.wait_ge(toep_in, 16)
            for h in range(HA):
                A.activation(Uh[:, h], U[:, h], ACT.Copy).then_inc(uh_ready, 1)
            for n in range(4):
                weights_b(n)
            for i in range(UNITS + 2):
                for u in range(BLK):
                    if 0 < i <= UNITS:
                        probabilities(i - 1, u)
                    if 1 < i <= UNITS + 1:
                        if u == 0:
                            unnormalised(i - 2, 1)
                        if u == 2:
                            normalised(i - 2, 0 if is_a(i - 2) else 1)
                    if i + 1 < BATCH and u in (0, 2, 4):
                        projected(i + 1, u // 2)
                    if BATCH <= i + 1 < UNITS and u in (3, 4, 5):
                        projected(i + 1, u - 3)
                    if 0 < i <= UNITS:
                        if u == 5:
                            unnormalised(i - 1, 0)
                        if not is_a(i - 1) and u == 7:
                            normalised(i - 1, 0)


def kernel(x, L0_conv_w_in, L0_conv_w_qk, L0_conv_w_out, L0_conv_rel_bias, L1_conv_w_qkv, L1_conv_w_out):
    import concourse.bacc as bacc
    from concourse.bass_utils import run_bass_kernel_spmd

    nc = bacc.Bacc("TRN2", target_bir_lowering=False, num_devices=1)
    consts, buckets = shape_constants()
    given = {
        "x": np.ascontiguousarray(x).reshape(BATCH, TOK, CH), "w_in": L0_conv_w_in, "w_qk": L0_conv_w_qk,
        "w_outa": L0_conv_w_out, "rel_bias": L0_conv_rel_bias, "w_qkv": L1_conv_w_qkv, "w_outb": L1_conv_w_out,
        "consts": consts, "buckets": buckets,
    }
    arrays = {name: np.ascontiguousarray(a) for name, a in given.items()}
    aps = {name: nc.dram_tensor(name, a.shape, mybir.dt.from_np(a.dtype), kind="ExternalInput").ap() for name, a in arrays.items()}
    out = nc.dram_tensor("y", (BATCH, TOK, CH), F32, kind="ExternalOutput").ap()
    build(nc, out=out, **aps)
    r = run_bass_kernel_spmd(nc, [arrays], core_ids=[0])
    return r.results[0]["y"].reshape(BATCH, HEIGHT, WIDTH, CH)
```

```python
import math
from contextlib import ExitStack

import numpy as np

import concourse.bass as bass
from concourse import mybir

F32 = mybir.dt.float32
F32R = mybir.dt.float32r
ALU = mybir.AluOpType
ACT = mybir.ActivationFunctionType
AX = mybir.AxisListType

P = 128
BATCH, HEIGHT, WIDTH, CH = 4, 16, 16, 256
TOK = HEIGHT * WIDTH
TT = TOK // P
CT = CH // P
HD = 16
HA = 8
HB = 16
CHUNK = 4 * WIDTH
NCH = TOK // CHUNK
GRP = 32
GC = CH // GRP
EPS = 1e-5
SCALE = HD ** -0.5
LOWEST = float(np.finfo(np.float32).min)
NBUCKET = 32
MAXDIST = 32
UNITS = 2 * BATCH
BLK = 8
BW = 512
TOEP = CH + P
NDIAG = 512

C_ID, C_GRP, C_SUB, C_HEAD, C_QUAD, C_HALF, C_PAIR, C_LOW = (0, P, 2 * P) + tuple(2 * P + HD + n for n in (0, 8, 12, 14, 18))
C_END = C_LOW + 1


def shape_constants():
    p = np.arange(P)
    c = np.zeros((P, C_END), np.float32)
    c[p, C_ID + p] = 1
    c[:, C_GRP:C_GRP + P] = (p[:, None] // GC == p[None, :] // GC) / GC
    c[p, C_SUB + p % HD] = 1
    c[p, C_HEAD + p // HD] = 1
    c[p, C_QUAD + p // HD % 4] = 1
    c[p, C_HALF + p // HD // 4] = 1
    c[p, C_PAIR + p // (2 * HD)] = 1
    c[:, C_LOW] = -(p // HD % 2)
    rel = 255 - np.arange(NDIAG)
    half, exact = NBUCKET // 2, NBUCKET // 4
    n = np.abs(rel)
    large = exact + (np.log(np.maximum(n, 1).astype(np.float32) / np.float32(exact))
                     / np.float32(math.log(MAXDIST / exact)) * np.float32(half - exact)).astype(np.int32)
    bucket = (rel >= 0) * half + np.where(n < exact, n, np.minimum(large, half - 1))
    return c, (np.arange(NBUCKET)[:, None] == bucket[None, :]).astype(np.float32)


def build(nc, x, w_in, w_qk, w_outa, rel_bias, w_qkv, w_outb, consts, buckets, out):
    with ExitStack() as ctx:
        def sb(name, shape, dt=F32):
            return ctx.enter_context(nc.sbuf_tensor(name, shape, dt))

        def sem(name):
            return ctx.enter_context(nc.semaphore(name))

        X = sb("X", [P, BATCH, TT, CH])
        Xn = sb("Xn", [P, BATCH, TT, CH])
        X1 = sb("X1", [P, BATCH, TT, CH])
        Xc, Sq = X1, Xn
        Part = sb("Part", [P, 2, BATCH, TT, GRP])
        Mu = sb("Mu", [P, BATCH, GRP])
        Sd = sb("Sd", [P, BATCH, GRP])
        Rs = sb("Rs", [P, BATCH, GRP])
        eps = sb("eps", [P, 1])
        warm = sb("warm", [P, 2])
        avg = sb("avg", [P, P])
        con = sb("con", [P, C_END])
        minus = sb("minus", [P, P], F32R)
        rb = sb("rb", [NBUCKET, HA])
        Km = sb("Km", [P, 2, 4, TOK], F32R)
        Tk = sb("Tk", [P, HA, TOEP])
        Tq = sb("Tq", [P, HA, TOEP])
        win = sb("win", [HA, HEIGHT])
        wouta = sb("wouta", [HEIGHT, HA])
        WinK = sb("WinK", [P, TT, P])
        WoutK = sb("WoutK", [P, TT, P])
        WQh, WQl, WKh, WKl = (sb(n, [P, 2, P], F32R) for n in ("WQh", "WQl", "WKh", "WKl"))
        WTh = sb("WTh", [P, CT, 3 * CH], F32R)
        WTl = sb("WTl", [P, CT, 3 * CH], F32R)
        WoT = sb("WoT", [P, 2, CH])
        XRh = sb("XRh", [P, CH], F32R)
        XRl = sb("XRl", [P, CH], F32R)
        QH = sb("QH", [P, 2, CH], F32R)
        QF = sb("QF", [P, 2, CH])
        KF = sb("KF", [P, 2, CH])
        Qst = sb("Qst", [P, 2, 2, CH], F32R)
        MRING = 11
        QM = sb("QM", [P, MRING, CH], F32R)
        KH = sb("KH", [P, 2, 2, CH], F32R)
        KL = sb("KL", [P, 2, 2, CH], F32R)
        VA = sb("VA", [P, 3, 2, HA, 32])
        XT = sb("XT", [P, CT, TOK])
        XTh = sb("XTh", [P, CT, TOK], F32R)
        XTl = sb("XTl", [P, CT, TOK], F32R)
        bst = sb("bst", [P, CT, 6])
        agg = sb("agg", [P, CT, 2])
        gm = sb("gm", [P, CT])
        dev = sb("dev", [P, CT])
        mom = sb("mom", [P, CT])
        gve = sb("gve", [P, CT])
        mhalf = sb("mhalf", [P, CT])
        grs = sb("grs", [P, CT])
        gnb = sb("gnb", [P, CT])
        KORDER = (0, 0, 1, 2, 3, 2, 1)
        WINDOW = (0, 1, 5, 3)
        Kf = sb("Kf", [P, 3, 2, len(KORDER) * CHUNK])
        Qn = sb("Qn", [P, 2, 2, TOK])
        Qs = sb("Qs", [P, 2, 2, NCH, 2, CHUNK], F32R)
        QRING = 3
        Qk = sb("Qk", [P, QRING, BW])
        VB = sb("VB", [P, 2, NCH, HB, 32])
        PT = sb("PT", [P, BLK, BW])
        room = Kf[:].rearrange("p a g n -> p (a g n)")
        wqkv = room[:, 0:6 * CH].rearrange("p (a c) -> p a c", c=CH)
        woutb = room[:, 6 * CH:8 * CH].rearrange("p (b c) -> p b c", c=CH)
        wins = PT[0:HA, 6, 0:HEIGHT * WIDTH].rearrange("h (c f) -> h c f", c=HEIGHT)
        woutas = PT[0:HEIGHT, 6, CH:CH + HA * HD].rearrange("c (h f) -> c h f", h=HA)
        wqk = PT[:, 7, 0:2 * P].rearrange("p (a c) -> p a c", a=2)
        hot, diag = PT[0:NBUCKET, 4, :], PT[0:HA, 5, :]
        NM = sb("NM", [P, 2, 32])
        DRING = 3
        D = sb("D", [P, DRING, BW], F32R)
        OS = sb("OS", [P, 2, BW])
        RC = sb("RC", [P, 2, 16])
        ON = sb("ON", [P, 2, 2, P])
        OT = sb("OT", [P, 2, 2, P])
        Y = sb("Y", [P, 2, CH])

        bank = [ctx.enter_context(nc.psum_tensor(f"bank{n}", [P, BW], F32)) for n in range(8)]
        S_BANK, Z_BANK, O_BANK, F_BANK, G_BANK = 0, 2, 4, 6, 7

        rows = nc.dram_tensor("bias_rows", (HA, NDIAG), F32, kind="Internal").ap()

        x_in = [sem(f"x_in{b}") for b in range(BATCH)]
        con_in, hot_in, rb_in, win_in, wouta_in = (sem(n) for n in ("con_in", "hot_in", "rb_in", "win_in", "wouta_in"))
        wqk_in, wqkv_in, woutb_in = sem("wqk_in"), sem("wqkv_in"), sem("woutb_in")
        rows_out = sem("rows_out")
        TPARTS = 4
        toep_in = [sem(f"toep_in{n}") for n in range(TPARTS)]
        y_out = [sem(f"y_out{half}") for half in range(2)]
        fills, dve_fills = sem("fills"), sem("dve_fills")
        rounded = sem("rounded")
        spread_ready = sem("spread_ready")
        small_done, small_ready = sem("small_done"), sem("small_ready")
        diag_done, diag_ready = sem("diag_done"), sem("diag_ready")
        wqk_done, wqk_ready = sem("wqk_done"), sem("wqk_ready")
        wb_done, wb_ready, wl_ready = sem("wb_done"), sem("wb_ready"), sem("wl_ready")
        tq_done, tq_ready = sem("tq_done"), sem("tq_ready")
        part_ready, mean_done, mu_ready = sem("part_ready"), sem("mean_done"), sem("mu_ready")
        cent_ready, cent_pool, sq_ready = sem("cent_ready"), sem("cent_pool"), sem("sq_ready")
        part2_ready, var_done, sd_ready, rs_ready = sem("part2_ready"), sem("var_done"), sem("sd_ready"), sem("rs_ready")
        xn_dve, xn_pool = sem("xn_dve"), sem("xn_pool")
        xr_done, xr_ready, xrl_ready = sem("xr_done"), sem("xr_ready"), sem("xrl_ready")
        q_done, k_done, v_done = sem("q_done"), sem("k_done"), sem("v_done")
        qh_ready, kh_ready, q_ready, k_ready, v_ready = (sem(n) for n in ("qh_ready", "kh_ready", "q_ready", "k_ready", "v_ready"))
        vx_ready = sem("vx_ready")
        xt_done, gm_done, gv_done, xt_ready, xf_ready, xl_ready = (sem(n) for n in ("xt_done", "gm_done", "gv_done", "xt_ready", "xf_ready", "xl_ready"))
        agg_ready, mom_ready, gve_ready, grs_ready, gnb_ready = (sem(n) for n in ("agg_ready", "mom_ready", "gve_ready", "grs_ready", "gnb_ready"))
        stat_step = sem("stat_step")
        s_done, max_ready, da_ready, d_ready = (sem(n) for n in ("s_done", "max_ready", "da_ready", "d_ready"))
        km_ready, qk_ready = sem("km_ready"), sem("qk_ready")
        zb_ready, qm_ready = sem("zb_ready"), sem("qm_ready")
        z_done, p_ready, pv_done, os_ready = sem("z_done"), sem("p_ready"), sem("pv_done"), sem("os_ready")
        t1_done, rc_ready, on_ready, t2_done, ot_ready, f_done = (sem(n) for n in ("t1_done", "rc_ready", "on_ready", "t2_done", "ot_ready", "f_done"))
        res_ready = sem("res_ready")

        block = ctx.enter_context(nc.Block())

        def is_a(i):
            return i < BATCH

        def halves(i):
            return i + 1 if is_a(i) else BATCH + 2 * (i - BATCH + 1)

        def grouped(t, b):
            return t[:, b].rearrange("p t (g c) -> p t g c", c=GC)

        def spread(t, b):
            return t[:, b].unsqueeze(1).unsqueeze(3).to_broadcast([P, TT, GRP, GC])

        def v_total(i):
            return i + 1 if is_a(i) else BATCH + 2 * (i - BATCH + 1)

        LAG = 4
        STEPS = UNITS * BLK + 12
        IN_A, IN_B = range(BATCH), range(BATCH, UNITS)
        XR_A, Q_A, K_A, V_A = -8, -6, -4, -2
        XT_B, GM_B, GV_B, Q_B, K_B, V_B = -9, -8, -7, -4, -3, -2
        FINISH = [(range(UNITS - 1), (10, 13), (12, 15), (13, 16), (15, 18)),
                  (range(UNITS - 1, UNITS), (10, 13), (12, 15), (13, 16), (14, 17))]

        def units_a(units):
            return [i for i in units if i in IN_A]

        def units_b(units):
            return [i for i in units if i in IN_B]

        def due(t, when, units):
            i, rest = divmod(t - when, BLK)
            return [i] if rest == 0 and i in units else []

        AHEAD = 2

        GROUPS = [(0, 1), (1, 2), (2, BATCH)]
        SUM_BANK = [O_BANK + 1, O_BANK, O_BANK + 1]

        @block.sync
        def _(sp):
            sp.dma_start(X[:, 0], x[0].rearrange("(t p) c -> p t c", p=P)).then_inc(x_in[0], 16)
            sp.dma_start(rb[:], rel_bias).then_inc(rb_in, 16)
            sp.dma_start(hot, buckets).then_inc(hot_in, 16)
            for b in range(1, BATCH):
                sp.dma_start(X[:, b], x[b].rearrange("(t p) c -> p t c", p=P)).then_inc(x_in[b], 16)
            sp.wait_ge(diag_ready, 1)
            sp.dma_start(rows, diag).then_inc(rows_out, 16)
            sp.wait_ge(rows_out, 16)
            for n in range(TPARTS):
                h0, h1 = n * HA // TPARTS, (n + 1) * HA // TPARTS
                sp.dma_start(Tk[:, h0:h1, :], bass.AP(rows.tensor, h0 * NDIAG, [[1, P], [NDIAG, h1 - h0], [1, TOEP]])).then_inc(toep_in[n], 16)
            sp.dma_start(wqkv, w_qkv.rearrange("(a p) c -> p a c", p=P)).then_inc(wqkv_in, 16)
            sp.dma_start(woutb, w_outb.rearrange("(a p) c -> p a c", p=P)).then_inc(woutb_in, 16)
            for i in range(BATCH, UNITS):
                for cp in range(2):
                    n = halves(i - 1) + cp + 1
                    sp.wait_ge(res_ready, n)
                    sp.dma_start(out[i - BATCH, cp * P:(cp + 1) * P, :], Y[:, cp]).then_inc(y_out[cp], 16)
            for half in range(2):
                sp.wait_ge(y_out[half], 16 * BATCH)

        @block.gpsimd
        def _(pool):
            pool.wait_ge(win_in, 16)
            nc.gpsimd.tensor_copy(wins, win[:].unsqueeze(2).to_broadcast([HA, HEIGHT, WIDTH])).then_inc(spread_ready, 1)
            pool.wait_ge(wouta_in, 16)
            nc.gpsimd.tensor_copy(woutas, wouta[:].unsqueeze(2).to_broadcast([HEIGHT, HA, HD])).then_inc(spread_ready, 1)
            nc.gpsimd.memset(VA[:, :, :, :, HD:], 1.0).then_inc(fills, 1)
            nc.gpsimd.memset(mhalf[:], -0.5).then_inc(fills, 1)
            for n in range(2):
                pool.wait_ge(fills, 2 + 3 * n)
                nc.gpsimd.memset(VB[:, n, 1:, :, HD:], 1.0).then_inc(fills, 1)
                pool.wait_ge(fills, 3 + 3 * n)
                nc.gpsimd.memset(VB[0:CHUNK, n, 0, :, HD:], 1.0).then_inc(fills, 1)
                pool.wait_ge(fills, 4 + 3 * n)
                nc.gpsimd.memset(VB[CHUNK:, n, 0], 0.0).then_inc(fills, 1)
            pool.wait_ge(fills, 8)

            def center(g):
                pool.wait_ge(mu_ready, g)
                for b in range(*GROUPS[g]):
                    nc.gpsimd.tensor_tensor(grouped(Xc, b), grouped(X, b), spread(Mu, b), op=ALU.subtract).then_inc(cent_pool, 1)

            def scale(g, b):
                pool.wait_ge(rs_ready, g + 1)
                nc.gpsimd.tensor_tensor(grouped(Xn, b)[:, :, ::-1, ::-1], grouped(Xc, b), spread(Rs, b), op=ALU.mult).then_inc(xn_pool, 1)

            def diagonal(i, u):
                idx = i * BLK + u
                pool.wait_ge(max_ready, idx + 1)
                if idx >= DRING:
                    pool.wait_ge(z_done, idx - DRING + 1)
                nc.gpsimd.tensor_tensor(D[:, idx % DRING, 0:CH].rearrange("p (h q) -> p h q", h=2),
                                        con[:, C_ID:C_ID + P].unsqueeze(1).to_broadcast([P, 2, P]),
                                        NM[:, i % 2, 2 * u:2 * u + 2].unsqueeze(2).to_broadcast([P, 2, P]), op=ALU.mult).then_inc(da_ready, 1)

            def high_and_low(i):
                pool.wait_ge(qh_ready, i + 1)
                if i >= 2:
                    pool.wait_ge(qm_ready, BLK * (i - 1))
                nc.gpsimd.tensor_tensor(Qst[:, i % 2], QF[:], QH[:].bitcast(F32), op=ALU.add).then_inc(q_ready, 1)

            def low_keys(i):
                pool.wait_ge(kh_ready, i + 1)
                nc.gpsimd.tensor_tensor(KL[:, i % 2], KF[:], KH[:, i % 2].bitcast(F32), op=ALU.subtract).then_inc(k_ready, 1)

            def head_queries(i, u):
                b, idx = i - BATCH, (i - BATCH) * BLK + u
                c, g = u // 2, u % 2
                if u == 0:
                    pool.wait_ge(qh_ready, i + 1)
                if idx >= QRING:
                    pool.wait_ge(z_done, i * BLK + u - QRING + 1)
                nc.gpsimd.tensor_tensor(
                    Qk[:, idx % QRING, :].rearrange("p (a v q) -> p v a q", a=4, v=2),
                    Qn[:, b % 2, g, c * CHUNK:(c + 1) * CHUNK].unsqueeze(1).unsqueeze(1).to_broadcast([P, 2, 4, CHUNK]),
                    con[:, C_HEAD:C_HEAD + 8].rearrange("p (v a) -> p v a", v=2).unsqueeze(3).to_broadcast([P, 2, 4, CHUNK]),
                    op=ALU.mult).then_inc(qk_ready, 1)

            def scale_b(b):
                if b:
                    pool.wait_ge(xf_ready, b)
                pool.wait_ge(gve_ready, b + 1)
                nc.gpsimd.tensor_tensor(grs[:], gve[:], mhalf[:], op=ALU.pow).then_inc(grs_ready, 1)

            def window_values(b, ahead):
                n = b % 2
                pool.wait_ge(v_ready, v_total(BATCH + b))
                pool.wait_ge(grs_ready, b + 1)
                if ahead < BATCH * BLK:
                    pool.wait_ge(da_ready, ahead + 1)
                else:
                    pool.wait_ge(qk_ready, ahead - BATCH * BLK + 1)
                nc.gpsimd.tensor_copy(VB[0:CHUNK, n, 0, :, 0:HD], VB[0:CHUNK, n, 1, :, 0:HD]).then_inc(vx_ready, 1)
                pool.wait_ge(vx_ready, 3 * b + 1)
                nc.gpsimd.tensor_copy(VB[0:CHUNK, n, 2, :, 0:HD], VB[0:CHUNK, n, 3, :, 0:HD]).then_inc(vx_ready, 1)
                pool.wait_ge(vx_ready, 3 * b + 2)
                nc.gpsimd.tensor_copy(VB[CHUNK:, n, 2, :, 0:HD], VB[CHUNK:, n, 1, :, 0:HD]).then_inc(vx_ready, 1)
                pool.wait_ge(vx_ready, 3 * b + 3)

            center(1)
            center(2)
            scale(1, 1)
            for t in range(STEPS):
                ahead = t - LAG + AHEAD
                if 0 <= ahead < BATCH * BLK:
                    diagonal(ahead // BLK, ahead % BLK)
                if BATCH * BLK <= ahead < UNITS * BLK:
                    head_queries(ahead // BLK, ahead % BLK)
                if t in (3, 4):
                    scale(2, t - 1)
                for i in due(t, Q_A + 1, IN_A[1:]):
                    high_and_low(i)
                for i in due(t, K_A + 1, IN_A[1:]):
                    low_keys(i)
                for i in due(t, GV_B, IN_B):
                    scale_b(i - BATCH)
                for i in due(t, V_B + 2, IN_B):
                    window_values(i - BATCH, ahead)

        @block.tensor
        def _(pe):
            ident = con[:, C_ID:C_ID + P]

            def small_weights():
                pe.wait_ge(con_in, 16)
                pe.wait_ge(spread_ready, 2)
                small = bank[Z_BANK]
                for t in range(TT):
                    lhs = wins[:, t * 8:(t + 1) * 8, :].rearrange("h c f -> h (c f)")
                    nc.tensor.matmul(small[:, t * HA:(t + 1) * HA], lhs, con[0:HA, C_ID:C_ID + HA], start=True, stop=True)
                lhs = woutas.rearrange("c h f -> c (h f)")
                nc.tensor.matmul(small[:, 64:64 + HEIGHT], lhs, con[0:HEIGHT, C_ID:C_ID + HEIGHT], start=True, stop=True).then_inc(small_done, 1)

            def bias_rows():
                pe.wait_ge(rb_in, 16)
                pe.wait_ge(hot_in, 16)
                nc.tensor.matmul(bank[Z_BANK + 1][0:HA, :], rb[:], hot, start=True, stop=True).then_inc(diag_done, 1)

            def query_key_weights():
                pe.wait_ge(con_in, 16)
                pe.wait_ge(wqk_in, 16)
                for a in range(2):
                    last = nc.tensor.transpose(bank[S_BANK][:, a * P:(a + 1) * P], wqk[:, a, :], ident)
                last.then_inc(wqk_done, 1)

            def query_bias(h):
                if h == 0:
                    pe.wait_ge(small_ready, 2)
                    pe.wait_ge(diag_ready, 1)
                pe.wait_ge(toep_in[h * TPARTS // HA], 16)
                if h >= 2:
                    pe.wait_ge(tq_ready, h - 1)
                for w in range(3):
                    last = nc.tensor.transpose(bank[Z_BANK + h % 2][:, w * P:(w + 1) * P], Tk[:, h, w * P:(w + 1) * P], ident)
                last.then_inc(tq_done, 1)

            def moments(g, which, ready, done):
                b0, b1 = GROUPS[g]
                pe.wait_ge(ready, g + 1)
                if g == 2:
                    pe.wait_ge(rs_ready, 1)
                col = 256 * which
                for t in range(TT):
                    last = nc.tensor.matmul(bank[SUM_BANK[g]][:, col:col + (b1 - b0) * GRP], avg[:],
                                            Part[:, which, b0:b1, t, :], start=(t == 0), stop=(t == TT - 1))
                last.then_inc(done, 1)

            def wait_bank_f(i):
                if i > 0:
                    if is_a(i - 1):
                        pe.wait_ge(k_ready if i == 1 else kh_ready, i)
                    else:
                        pe.wait_ge(kh_ready, i)

            def project_a(i, step):
                f = bank[G_BANK if step % 2 else F_BANK]
                if step == 0:
                    if i == 0:
                        pe.wait_ge(xn_dve, 1)
                        pe.wait_ge(small_ready, 2)
                    else:
                        pe.wait_ge(xn_pool, i)
                    wait_bank_f(i)
                    for t in range(TT):
                        last = nc.tensor.matmul(f[:, 0:CH], WinK[:, t, :], Xn[:, i, t, :], start=(t == 0), stop=(t == TT - 1))
                    last.then_inc(xr_done, 1)
                if step == 1:
                    if i == 0:
                        pe.wait_ge(wqk_ready, 4)
                    else:
                        pe.wait_ge(v_ready, v_total(i - 1))
                    pe.wait_ge(xr_ready, i + 1)
                    for n, (w, v) in enumerate(((WQh, XRh), (WQl, XRh), (WQh, XRl))):
                        if v is XRl:
                            pe.wait_ge(xrl_ready, i + 1)
                        for t in range(2):
                            last = nc.tensor.matmul(f[:, t * CH:(t + 1) * CH], w[:, t, :], v[:, ::-1],
                                                    start=(n + t == 0), stop=(n == 2), skip_group_check=True)
                    last.then_inc(q_done, 1)
                if step == 2:
                    for n, (w, v) in enumerate(((WKh, XRh), (WKl, XRh), (WKh, XRl))):
                        for t in range(2):
                            last = nc.tensor.matmul(f[:, t * CH:(t + 1) * CH], w[:, t, :], v[:],
                                                    start=(n + t == 0), stop=(n == 2), skip_group_check=True)
                    last.then_inc(k_done, 1)
                if step == 3:
                    pe.wait_ge(qh_ready if i else q_ready, i + 1)
                    for m in range(2):
                        for t in range(TT):
                            last = nc.tensor.matmul(f[:, m * P:(m + 1) * P], Xn[:, i, t, m * P:(m + 1) * P], WinK[:, t, :],
                                                    start=(t == 0), stop=(t == TT - 1))
                    last.then_inc(v_done, 1)

            def project_b(i, step):
                b = i - BATCH
                f, m = bank[F_BANK], bank[G_BANK]
                if step == 0:
                    pe.wait_ge(res_ready, b + 1)
                    wait_bank_f(i)
                    for k in range(CT):
                        for t in range(TT):
                            last = nc.tensor.transpose(f[:, k * TOK + t * P:k * TOK + (t + 1) * P],
                                                       X1[:, b, t, k * P:(k + 1) * P], ident)
                    last.then_inc(xt_done, 1)
                if step == 1:
                    pe.wait_ge(agg_ready, b + 1)
                    pe.wait_ge(v_ready, v_total(i - 1))
                    nc.tensor.matmul(m[:, 0:CT], con[:, C_GRP:C_GRP + P], agg[:, :, 0], start=True, stop=True).then_inc(gm_done, 1)
                if step == 2:
                    pe.wait_ge(mom_ready, b + 1)
                    nc.tensor.matmul(m[:, 4:4 + CT], con[:, C_GRP:C_GRP + P], mom[:], start=True, stop=True).then_inc(gv_done, 1)
                if step in (3, 4):
                    if step == 3:
                        f = m
                        pe.wait_ge(gve_ready, b + 1)
                        pe.wait_ge(xt_ready, b + 1)
                        pe.wait_ge(wl_ready, 3)
                    else:
                        pe.wait_ge(xf_ready, b + 1)
                    for n, (w, v) in enumerate(((WTh, XTh), (WTl, XTh), (WTh, XTl))):
                        if step == 3 and v is XTl:
                            pe.wait_ge(xl_ready, b + 1)
                        for g in range(2):
                            for k in range(CT):
                                col = (step - 3) * CH + g * P
                                last = nc.tensor.matmul(f[:, g * TOK:(g + 1) * TOK], w[:, k, col:col + P], v[:, k, :],
                                                        start=(n + g + k == 0), stop=(n == 2 and k == CT - 1), skip_group_check=True)
                    last.then_inc(q_done if step == 3 else k_done, 1)
                if step == 5:
                    f = m
                    pe.wait_ge(qh_ready, i + 1)
                    for n, (w, v) in enumerate(((WTh, XTh), (WTl, XTh), (WTh, XTl))):
                        for t in range(TT):
                            for k in range(CT):
                                last = nc.tensor.matmul(f[:, t * CH:(t + 1) * CH], v[:, k, t * P:(t + 1) * P], w[:, k, 2 * CH:],
                                                        start=(n + t + k == 0), stop=(n == 2 and k == CT - 1), skip_group_check=True)
                    last.then_inc(v_done, 1)

            def scores_a(i, u):
                s = bank[S_BANK + u % 2]
                queries = QM[:, (i * BLK + u) % MRING, :]
                pe.wait_ge(qm_ready, i * BLK + u + 1)
                for nt in range(2):
                    last = nc.tensor.matmul(s[:, nt * CH:(nt + 1) * CH], queries[:, nt * P:(nt + 1) * P], KH[:, i % 2, u // 4, :], start=(nt == 0), stop=(nt == 1), skip_group_check=True)
                return last

            def scores_b(i, u):
                b = i - BATCH
                c, g = u // 2, u % 2
                if u < 2:
                    pe.wait_ge(km_ready, 2 * b + g + 1)
                keys = Km[:, g, :, :]
                if c == 0:
                    rhs = keys[:, :, 0:CHUNK].unsqueeze(2).to_broadcast([P, 4, 2, CHUNK])
                else:
                    rhs = keys[:, :, (c - 1) * CHUNK:(c + 1) * CHUNK]
                return nc.tensor.matmul(bank[S_BANK + u % 2][:], Qs[:, b % 2, g, c].rearrange("p v q -> p (v q)"), rhs,
                                        start=True, stop=True)

            def shifted_a(i, u):
                z = bank[Z_BANK + u % 2]
                n, q = i % 2, u // 4
                zs = z[:].rearrange("p (s n) -> p s n", s=2)
                nc.tensor.matmul(z[:], minus[:], D[:, (i * BLK + u) % DRING, 0:CH].unsqueeze(1).to_broadcast([P, 2, CH]),
                                 start=True, stop=False, skip_group_check=True)
                for s in range(2):
                    for keys in (KH, KL):
                        last = nc.tensor.matmul(zs[:, s, :], keys[:, n, q, s * P:(s + 1) * P], QM[:, (i * BLK + u) % MRING, :],
                                                start=False, stop=(s == 1 and keys is KL), skip_group_check=True)
                return last

            def shifted_b(i, u):
                z = bank[Z_BANK + u % 2]
                b = i - BATCH
                c, g = u // 2, u % 2
                nc.tensor.matmul(z[:], minus[:], D[:, (i * BLK + u) % DRING, :], start=True, stop=False, skip_group_check=True)
                pe.wait_ge(qk_ready, b * BLK + u + 1)
                w = WINDOW[c] * CHUNK
                return nc.tensor.matmul(z[:], Kf[:, b % 3, g, w:w + 2 * CHUNK], Qk[:, (b * BLK + u) % QRING, :],
                                        start=False, stop=True, skip_group_check=True)

            def scores(i, u):
                idx = i * BLK + u
                if u == 0:
                    pe.wait_ge(q_ready, i + 1)
                    if is_a(i):
                        pe.wait_ge(kh_ready, i + 1)
                if idx >= 2:
                    pe.wait_ge(max_ready, idx - 1)
                (scores_a if is_a(i) else scores_b)(i, u).then_inc(s_done, 1)

            def shifted(i, u):
                idx = i * BLK + u
                if is_a(i):
                    pe.wait_ge(da_ready, idx + 1)
                else:
                    pe.wait_ge(d_ready, idx - BATCH * BLK + 1)
                if u == 0:
                    pe.wait_ge(k_ready if is_a(i) else kh_ready, i + 1)
                if idx >= 2:
                    pe.wait_ge(p_ready, idx - 1)
                (shifted_a if is_a(i) else shifted_b)(i, u).then_inc(z_done, 1)

            def values(i, half):
                o = bank[O_BANK + half]
                pe.wait_ge(p_ready, i * BLK + 4 * (half + 1))
                if half == 0:
                    if is_a(i):
                        pe.wait_ge(v_ready, v_total(i))
                        if i == 0:
                            pe.wait_ge(fills, 1)
                    else:
                        pe.wait_ge(vx_ready, 3 * (i - BATCH + 1))
                    if i == 0:
                        pe.wait_ge(wb_ready, 4)
                        pe.wait_ge(rs_ready, 3)
                if i > 0:
                    if half == 1 or not is_a(i - 1):
                        pe.wait_ge(res_ready, halves(i - 1) - (0 if is_a(i - 1) else 1 - half))
                    else:
                        pe.wait_ge(ot_ready, halves(i - 1))
                if is_a(i):
                    for mt in range(2):
                        for hh in range(4):
                            last = nc.tensor.matmul(o[32 * hh:32 * hh + 32, 0:CH], VA[:, i % 3, mt, 4 * half + hh, :],
                                                    PT[:, 4 * half + hh, mt * CH:(mt + 1) * CH],
                                                    start=(mt == 0), stop=(mt == 1))
                else:
                    for j in range(4):
                        for c2 in range(2):
                            for hh in range(4):
                                h = 4 * j + hh
                                col = j * P + c2 * CHUNK
                                last = nc.tensor.matmul(o[32 * hh:32 * hh + 32, col:col + CHUNK],
                                                        VB[:, (i - BATCH) % 2, 2 * half + c2, h, :],
                                                        PT[:, 4 * half + 2 * c2 + j // 2, hh * P + j % 2 * CHUNK:hh * P + (j % 2 + 1) * CHUNK],
                                                        start=True, stop=True)
                last.then_inc(pv_done, 1)

            def finish(i, half, step):
                n = halves(i - 1) + (half if not is_a(i) else 0) if i else 0
                o = bank[O_BANK + half]
                if step == 0:
                    if is_a(i):
                        pe.wait_ge(os_ready, 2 * (i + 1))
                        for nt in range(2):
                            for q in range(2):
                                col = (2 * nt + q) * P
                                last = nc.tensor.transpose(o[:, col:col + P], OS[:, q, nt * P:(nt + 1) * P], ident)
                    else:
                        pe.wait_ge(os_ready, 2 * i + half + 1)
                        for j in range(4):
                            last = nc.tensor.transpose(o[:, j * P:(j + 1) * P], OS[:, half, j * P:(j + 1) * P], ident)
                    last.then_inc(t1_done, 1)
                if step == 1:
                    pe.wait_ge(on_ready, n + 1)
                    t2 = o
                    for k in range(2):
                        src = ON[:, k, 0, :] if is_a(i) else ON[:, half, k, :]
                        last = nc.tensor.transpose(t2[:, k * P:(k + 1) * P], src, ident)
                    last.then_inc(t2_done, 1)
                if step == 2:
                    pe.wait_ge(ot_ready, n + 1)
                    if is_a(i):
                        for t in range(TT):
                            last = nc.tensor.matmul(bank[O_BANK + 1][:, t * CH:(t + 1) * CH], WoutK[:, t, :],
                                                    OT[:, 0, :, :].rearrange("p a b -> p (a b)"), start=True, stop=True)
                    else:
                        for g in range(2):
                            last = nc.tensor.matmul(o[:, 0:CH], OT[:, half, g, :], WoT[:, g, :], start=(g == 0), stop=(g == 1))
                    last.then_inc(f_done, 1)

            def weights_b(n):
                if n == 0:
                    pe.wait_ge(wqkv_in, 16)
                    pe.wait_ge(rs_ready, 2)
                else:
                    pe.wait_ge(wl_ready, n)
                if n == 3:
                    pe.wait_ge(woutb_in, 16)
                for m in range(4):
                    if n < 3:
                        src = wqkv[:, 2 * n + m % 2, (m // 2) * P:(m // 2 + 1) * P]
                    else:
                        src = woutb[:, m % 2, (m // 2) * P:(m // 2 + 1) * P]
                    last = nc.tensor.transpose(bank[O_BANK][:, m * P:(m + 1) * P], src, ident)
                last.then_inc(wb_done, 1)

            pe.wait_ge(dve_fills, 1)
            moments(0, 0, part_ready, mean_done)
            bias_rows()
            query_key_weights()
            moments(0, 1, part2_ready, var_done)
            small_weights()
            moments(1, 0, part_ready, mean_done)
            project_a(0, 0)
            moments(2, 0, part_ready, mean_done)
            project_a(0, 1)
            project_a(0, 2)
            query_bias(0)
            query_bias(1)
            moments(1, 1, part2_ready, var_done)
            pe.wait_ge(rounded, 1)
            for t in range(STEPS):
                if t < UNITS * BLK:
                    scores(t // BLK, t % BLK)
                if 0 <= t - LAG < UNITS * BLK:
                    shifted((t - LAG) // BLK, (t - LAG) % BLK)
                if t < 3:
                    query_bias(2 * t + 2)
                    query_bias(2 * t + 3)
                if t == 0:
                    project_a(0, 3)
                if t == 1:
                    moments(2, 1, part2_ready, var_done)
                if t in (4, 5, 7, 9):
                    weights_b((4, 5, 7, 9).index(t))
                for step, when in enumerate((XR_A, Q_A, K_A, V_A)):
                    for i in due(t, when, IN_A[1:]):
                        project_a(i, step)
                for step, when in enumerate((XT_B, GM_B, GV_B, Q_B, K_B, V_B)):
                    for i in due(t, when, IN_B):
                        project_b(i, step)
                for units, pv, *steps in FINISH:
                    for half in range(2):
                        for step, when in enumerate(steps):
                            for i in due(t, when[half], units_b(units)):
                                finish(i, half, step)
                    for step, when in enumerate(steps):
                        for i in due(t, when[1], units_a(units)):
                            finish(i, 0, step)
                    for half in range(2):
                        for i in due(t, pv[half], units):
                            values(i, half)

        @block.vector
        def _(dve):
            V = nc.vector
            V.memset(avg[:], 1.0 / (TOK * GC)).then_inc(dve_fills, 1)
            V.memset(eps[:], EPS).then_inc(dve_fills, 1)

            def part_sums(g, src, which, done):
                b0, b1 = GROUPS[g]
                V.tensor_reduce(Part[:, which, b0:b1].rearrange("p b t g -> p (b t g)"),
                                src[:, b0:b1].rearrange("p b t (g c) -> p (b t g) c", c=GC), AX.X, ALU.add).then_inc(done, 1)

            def norm_x(g, step):
                b0, b1 = GROUPS[g]
                m = bank[SUM_BANK[g]]
                if step == 0:
                    for b in range(b0, b1):
                        dve.wait_ge(x_in[b], 16)
                    part_sums(g, X, 0, part_ready)
                if step == 1:
                    dve.wait_ge(mean_done, g + 1)
                    if g == 0:
                        mean = m[:, 0:GRP].unsqueeze(1).unsqueeze(3).to_broadcast([P, TT, GRP, GC])
                        V.tensor_tensor(grouped(Xc, 0), grouped(X, 0), mean, op=ALU.subtract).then_inc(cent_ready, 1)
                    else:
                        V.tensor_copy(Mu[:, b0:b1].rearrange("p b g -> p (b g)"), m[:, 0:(b1 - b0) * GRP]).then_inc(mu_ready, 1)
                if step == 2:
                    dve.wait_ge(sq_ready, b1)
                    part_sums(g, Sq, 1, part2_ready)
                if step == 3:
                    dve.wait_ge(sd_ready, g + 1)
                    V.reciprocal(Rs[:, b0:b1], Sd[:, b0:b1]).then_inc(rs_ready, 1)
                    if g == 0:
                        dve.wait_ge(rs_ready, 1)
                        V.tensor_tensor(grouped(Xn, 0)[:, :, ::-1, ::-1], grouped(Xc, 0), spread(Rs, 0), op=ALU.mult).then_inc(xn_dve, 1)

            def small_weights():
                dve.wait_ge(con_in, 16)
                dve.wait_ge(small_done, 1)
                sub = con[:, C_SUB:C_SUB + HD]
                small = bank[Z_BANK]
                V.tensor_tensor(WinK[:].rearrange("p t (h f) -> p (t h) f", f=HD),
                                small[:, 0:TT * HA].unsqueeze(2).to_broadcast([P, TT * HA, HD]),
                                sub.unsqueeze(1).to_broadcast([P, TT * HA, HD]), op=ALU.mult).then_inc(small_ready, 1)
                V.tensor_tensor(WoutK[:].rearrange("p t (c f) -> p (t c) f", f=WIDTH),
                                small[:, 64:64 + HEIGHT].unsqueeze(2).to_broadcast([P, HEIGHT, WIDTH]),
                                sub.unsqueeze(1).to_broadcast([P, HEIGHT, WIDTH]), op=ALU.mult).then_inc(small_ready, 1)

            def query_key_weights():
                dve.wait_ge(wqk_done, 1)
                for k, (high, low) in enumerate(((WQh, WQl), (WKh, WKl))):
                    src = bank[S_BANK][:, 0:2 * P].rearrange("p (h k d) -> p h k d", k=2, d=HD)[:, :, k, :]
                    src = src.unsqueeze(2).to_broadcast([P, HA, 2, HD])
                    high, low = (w[:].rearrange("p t (h r d) -> p (t h) r d", r=2, d=HD) for w in (high, low))
                    V.tensor_copy(high, src).then_inc(wqk_ready, 1)
                    dve.wait_ge(wqk_ready, 2 * k + 1)
                    V.tensor_tensor(low, src, high.bitcast(F32), op=ALU.subtract).then_inc(wqk_ready, 1)

            def low_xr(i):
                dve.wait_ge(xr_ready, i + 1)
                if i:
                    dve.wait_ge(k_done, i)
                V.tensor_tensor(XRl[:], bank[F_BANK][:, 0:CH], XRh[:].bitcast(F32), op=ALU.subtract).then_inc(xrl_ready, 1)

            def queries_keys(i, which):
                if is_a(i):
                    f = bank[G_BANK if which == 0 else F_BANK]
                    if which == 0:
                        dve.wait_ge(qh_ready, i + 1)
                        V.tensor_tensor(Qst[:, i % 2].rearrange("p t n -> p (t n)"), f[:],
                                        QH[:].rearrange("p t n -> p (t n)").bitcast(F32), op=ALU.add).then_inc(q_ready, 1)
                    else:
                        dve.wait_ge(kh_ready, i + 1)
                        V.tensor_tensor(KL[:, i % 2].rearrange("p t n -> p (t n)"), f[:],
                                        KH[:, i % 2].rearrange("p t n -> p (t n)").bitcast(F32), op=ALU.subtract).then_inc(k_ready, 1)
                else:
                    b = i - BATCH
                    if which == 0:
                        dve.wait_ge(qh_ready, i + 1)
                        if b >= 2:
                            dve.wait_ge(s_done, BLK * (i - 1))
                        for v in range(2):
                            last = V.tensor_scalar(Qs[:, b % 2, :, :, v, :], Qn[:, b % 2].rearrange("p g (c q) -> p g c q", c=NCH),
                                                   con[:, C_HALF + v:C_HALF + v + 1], None, ALU.mult)
                        last.then_inc(q_ready, 1)

            def low_weights(n):
                dve.wait_ge(wb_ready, n + 1)
                src = bank[O_BANK][:].rearrange("p (k r) -> p k r", k=2)
                V.tensor_tensor(WTl[:, :, n * CH:(n + 1) * CH], src, WTh[:, :, n * CH:(n + 1) * CH].bitcast(F32),
                                op=ALU.subtract).then_inc(wl_ready, 1)

            def low_x(b):
                dve.wait_ge(xf_ready, b + 1)
                if b:
                    dve.wait_ge(v_done, BATCH + b)
                V.tensor_tensor(XTl[:], XT[:], XTh[:].bitcast(F32), op=ALU.subtract).then_inc(xl_ready, 1)

            def value_rows(i):
                f = bank[G_BANK]
                dve.wait_ge(v_done, i + 1)
                if is_a(i):
                    if i >= 3:
                        dve.wait_ge(pv_done, 2 * (i - 2))
                    V.tensor_copy(VA[:, i % 3, :, :, 0:HD], f[:, 0:2 * P].rearrange("p (m h d) -> p m h d", m=2, d=HD)).then_inc(v_ready, 1)
                else:
                    b = i - BATCH
                    if b == 0:
                        dve.wait_ge(fills, 8)
                    if b >= 2:
                        dve.wait_ge(pv_done, 2 * (i - 1))
                        dve.wait_ge(vx_ready, 3 * (b - 1))
                    for t in range(TT):
                        V.tensor_copy(VB[:, b % 2, 2 * t + 1, :, 0:HD],
                                      f[:, t * CH:(t + 1) * CH].rearrange("p (h d) -> p h d", d=HD)).then_inc(v_ready, 1)

            def norm_b(b, step):
                m = bank[G_BANK]
                c0 = 4 * b
                if step == 0:
                    dve.wait_ge(xt_done, b + 1)
                    for k in range(CT):
                        V.bn_stats(bst[:, k, :], bank[F_BANK][:, k * TOK:(k + 1) * TOK]).then_inc(stat_step, 1)
                    dve.wait_ge(stat_step, c0 + 2)
                    if b:
                        dve.wait_ge(gm_done, b)
                    for k in range(CT):
                        last = V.bn_aggr(agg[:, k, :], bst[:, k, :])
                    last.then_inc(agg_ready, 1)
                if step == 1:
                    dve.wait_ge(gm_done, b + 1)
                    dve.wait_ge(agg_ready, b + 1)
                    V.tensor_tensor(dev[:], agg[:, :, 0], m[:, 0:CT], op=ALU.subtract).then_inc(stat_step, 1)
                    V.tensor_copy(gm[:], m[:, 0:CT]).then_inc(stat_step, 1)
                    dve.wait_ge(stat_step, c0 + 3)
                    for k in range(CT):
                        last = V.scalar_tensor_tensor(mom[:, k:k + 1], dev[:, k:k + 1], dev[:, k:k + 1], agg[:, k, 1:2], ALU.mult, ALU.add)
                    last.then_inc(mom_ready, 1)
                if step == 2:
                    dve.wait_ge(gv_done, b + 1)
                    V.tensor_scalar(gve[:], m[:, 4:4 + CT], EPS, None, ALU.add).then_inc(gve_ready, 1)
                if step == 3:
                    dve.wait_ge(grs_ready, b + 1)
                    V.scalar_tensor_tensor(gnb[:], gm[:], -1.0, grs[:], ALU.mult, ALU.mult).then_inc(gnb_ready, 1)

            def block_max(i, u):
                dve.wait_ge(s_done, i * BLK + u + 1)
                s = bank[S_BANK + u % 2]
                if i >= 2 and is_a(i - 2):
                    dve.wait_ge(da_ready, (i - 2) * BLK + u + 1)
                elif i >= 2:
                    dve.wait_ge(d_ready, (i - 2 - BATCH) * BLK + u + 1)
                if is_a(i):
                    if i == 0:
                        dve.wait_ge(tq_ready, u + 1)
                    for nt in range(2):
                        half = s[:, nt * CH:(nt + 1) * CH]
                        last = V.tensor_tensor_reduce(half, half, Tq[:, u, nt * P:nt * P + CH],
                                                      1.0, LOWEST, ALU.add, ALU.max, NM[:, i % 2, 2 * u + nt:2 * u + nt + 1])
                    last.then_inc(max_ready, 1)
                else:
                    V.tensor_reduce(NM[:, i % 2, 4 * u:4 * u + 4], s[:].rearrange("p (h m) -> p h m", h=4), AX.X, ALU.max).then_inc(max_ready, 1)

            def diagonal(i, u):
                idx = i * BLK + u
                n = 4
                dve.wait_ge(max_ready, idx + 1)
                dve.wait_ge(z_done, idx - DRING + 1)
                V.tensor_tensor(D[:, idx % DRING, 0:n * P].rearrange("p (h q) -> p h q", h=n),
                                con[:, C_ID:C_ID + P].unsqueeze(1).to_broadcast([P, n, P]),
                                NM[:, i % 2, n * u:n * u + n].unsqueeze(2).to_broadcast([P, n, P]), op=ALU.mult).then_inc(d_ready, 1)

            def biased(i, u):
                z = bank[Z_BANK + u % 2][:].rearrange("p (s n) -> p s n", s=2)
                dve.wait_ge(z_done, i * BLK + u + 1)
                strip = Tk[:, u, :]
                strip = bass.AP(strip.tensor, strip.offset, [strip.ap[0], [P, 2], [1, CH]])
                V.tensor_tensor(z, z, strip, op=ALU.add).then_inc(zb_ready, 1)

            def divide(i, half):
                n = (halves(i - 1) if i else 0) + (0 if is_a(i) else half)
                o = bank[O_BANK + half]
                dve.wait_ge(t1_done, n + 1)
                V.reciprocal(RC[:, half, :], o[:].rearrange("p (a z) -> p a z", z=32)[:, :, HD]).then_inc(rc_ready, 1)
                dve.wait_ge(rc_ready, n + 1)
                if is_a(i):
                    V.tensor_tensor(ON[:, :, 0, :].rearrange("p n (h d) -> p n h d", d=HD),
                                    o[:].rearrange("p (n h z) -> p n h z", n=2, z=32)[:, :, :, 0:HD],
                                    RC[:, half, :].rearrange("p (n h) -> p n h", n=2).unsqueeze(3).to_broadcast([P, 2, HA, HD]),
                                    op=ALU.mult).then_inc(on_ready, 1)
                else:
                    V.tensor_tensor(ON[:, half].rearrange("p g (h d) -> p (g h) d", d=HD),
                                    o[:].rearrange("p (h z) -> p h z", z=32)[:, :, 0:HD],
                                    RC[:, half, :].unsqueeze(2).to_broadcast([P, HB, HD]), op=ALU.mult).then_inc(on_ready, 1)

            def residual(i, half):
                n = (halves(i - 1) if i else 0) + (0 if is_a(i) else half)
                o = bank[O_BANK + 1] if is_a(i) else bank[O_BANK + half]
                dve.wait_ge(f_done, n + 1)
                if is_a(i):
                    V.tensor_tensor(X1[:, i].rearrange("p t c -> p (t c)"), o[:], X[:, i].rearrange("p t c -> p (t c)"),
                                    op=ALU.add).then_inc(res_ready, 1)
                else:
                    b = i - BATCH
                    if b:
                        dve.wait_ge(y_out[half], 16 * b)
                    V.tensor_tensor(Y[:, half], o[:, 0:CH], X1[:, b, half, :], op=ALU.add).then_inc(res_ready, 1)

            norm_x(0, 0)
            norm_x(0, 1)
            dve.wait_ge(diag_done, 1)
            V.tensor_copy(diag, bank[Z_BANK + 1][0:HA, :]).then_inc(diag_ready, 1)
            norm_x(0, 2)
            norm_x(1, 0)
            query_key_weights()
            norm_x(0, 3)
            small_weights()
            norm_x(1, 1)
            norm_x(2, 0)
            V.tensor_scalar(minus[:], con[:, C_ID:C_ID + P], 0.0, -1.0, ALU.mult, ALU.add).then_inc(rounded, 1)
            low_xr(0)
            norm_x(2, 1)
            norm_x(1, 2)
            queries_keys(0, 0)
            queries_keys(0, 1)
            norm_x(1, 3)
            for t in range(STEPS):
                ahead = t - LAG + AHEAD
                if BATCH * BLK <= ahead < UNITS * BLK:
                    diagonal(ahead // BLK, ahead % BLK)
                if t < UNITS * BLK:
                    block_max(t // BLK, t % BLK)
                if 0 <= t - LAG < BATCH * BLK:
                    biased((t - LAG) // BLK, (t - LAG) % BLK)
                if t == 0:
                    norm_x(2, 2)
                    value_rows(0)
                if t == 1:
                    norm_x(2, 3)
                for i in due(t, V_A + 1, IN_A[1:]) + due(t, V_B + 1, IN_B):
                    value_rows(i)
                for step, when in enumerate((XT_B, GM_B, GV_B, GV_B + 1)):
                    for i in due(t, when, IN_B):
                        norm_b(i - BATCH, step)
                for i in due(t, XR_A + 1, IN_A[1:]):
                    low_xr(i)
                for i in due(t, GV_B + 2, IN_B):
                    low_x(i - BATCH)
                if t in (4, 5, 7):
                    low_weights((4, 5, 7).index(t))
                for i in due(t, Q_B + 1, IN_B):
                    queries_keys(i, 0)
                for units, pv, t1, t2, out_step in FINISH:
                    for half in range(2):
                        for i in due(t, t1[half], units_b(units)):
                            divide(i, half)
                        for i in due(t, out_step[half] + 1, units_b(units)):
                            residual(i, half)
                    for i in due(t, t1[1], units_a(units)):
                        divide(i, 0)
                    for i in due(t, out_step[1] + 1, units_a(units)):
                        residual(i, 0)

        @block.scalar
        def _(act):
            A = nc.scalar
            act.dma_start(con[:], consts).then_inc(con_in, 16)
            act.dma_start(win[:], w_in).then_inc(win_in, 16)
            act.dma_start(wouta[:], w_outa).then_inc(wouta_in, 16)
            act.dma_start(wqk, w_qk.rearrange("(a p) c -> p a c", p=P)).then_inc(wqk_in, 16)
            act.wait_ge(dve_fills, 2)
            A.activation(warm[:, 0:1], eps[:], ACT.Sqrt)

            def squares(b):
                if b == 0:
                    act.wait_ge(cent_ready, 1)
                else:
                    act.wait_ge(cent_pool, b)
                A.activation(Sq[:, b], Xc[:, b], ACT.Square).then_inc(sq_ready, 1)

            def deviation(g):
                b0, b1 = GROUPS[g]
                act.wait_ge(var_done, g + 1)
                A.activation(Sd[:, b0:b1].rearrange("p b g -> p (b g)"), bank[SUM_BANK[g]][:, 256:256 + (b1 - b0) * GRP],
                             ACT.Sqrt, bias=eps[:]).then_inc(sd_ready, 1)

            def weights_b(n):
                act.wait_ge(wb_done, n + 1)
                src = bank[O_BANK][:].rearrange("p (k r) -> p k r", k=2)
                dst = WTh[:, :, n * CH:(n + 1) * CH] if n < 3 else WoT[:]
                A.activation(dst, src, ACT.Copy).then_inc(wb_ready, 1)

            def projected(i, which):
                f = bank[G_BANK if which == 1 else F_BANK]
                if is_a(i):
                    if which == 0:
                        act.wait_ge(xr_done, i + 1)
                        if i:
                            act.wait_ge(k_done, i)
                        A.activation(XRh[:], f[:, 0:CH], ACT.Copy).then_inc(xr_ready, 1)
                    if which == 1:
                        act.wait_ge(q_done, i + 1)
                        if i:
                            act.wait_ge(q_ready, i)
                        last = A.activation(QH[:].rearrange("p t n -> p (t n)"), f[:], ACT.Copy, scale=con[:, C_LOW:C_LOW + 1])
                        if i:
                            last = A.activation(QF[:].rearrange("p t n -> p (t n)"), f[:], ACT.Copy)
                        last.then_inc(qh_ready, 1)
                    if which == 2:
                        act.wait_ge(k_done, i + 1)
                        if i >= 2:
                            act.wait_ge(z_done, BLK * (i - 1))
                            act.wait_ge(k_ready, i)
                        last = A.activation(KH[:, i % 2].rearrange("p t n -> p (t n)"), f[:], ACT.Copy)
                        if i:
                            last = A.activation(KF[:].rearrange("p t n -> p (t n)"), f[:], ACT.Copy)
                        last.then_inc(kh_ready, 1)
                else:
                    b = i - BATCH
                    if which == 0:
                        act.wait_ge(gnb_ready, b + 1)
                        if b:
                            act.wait_ge(v_done, i)
                        for dst, ready in ((XTh, xt_ready), (XT, xf_ready)):
                            for k in range(CT):
                                last = A.activation(dst[:, k, :], f[:, k * TOK:(k + 1) * TOK], ACT.Identity,
                                                    bias=gnb[:, k:k + 1], scale=grs[:, k:k + 1])
                            last.then_inc(ready, 1)
                    if which == 1:
                        act.wait_ge(q_done, i + 1)
                        if b >= 2:
                            act.wait_ge(qk_ready, BLK * (b - 1))
                        A.activation(Qn[:, b % 2].rearrange("p g n -> p (g n)"), f[:], ACT.Copy).then_inc(qh_ready, 1)
                    if which == 2:
                        act.wait_ge(k_done, i + 1)
                        if b >= 3:
                            act.wait_ge(z_done, BLK * (i - 2))
                        src = f[:].rearrange("p (g n) -> p g n", g=2)
                        for slot, c, m in ((0, 0, 1), (1, 0, 4), (5, 2, 1), (6, 1, 1)):
                            last = A.activation(Kf[:, b % 3, :, slot * CHUNK:(slot + m) * CHUNK],
                                                src[:, :, c * CHUNK:(c + m) * CHUNK], ACT.Copy)
                        last.then_inc(kh_ready, 1)

            def head_queries(i, u):
                idx = i * BLK + u
                if u == 0:
                    act.wait_ge(q_ready, i + 1)
                if idx >= MRING:
                    act.wait_ge(z_done, idx - MRING + 1)
                A.activation(QM[:, idx % MRING, :], Qst[:, i % 2, u // 4, :].bitcast(F32), ACT.Copy,
                             scale=con[:, C_PAIR + u % 4:C_PAIR + u % 4 + 1]).then_inc(qm_ready, 1)

            def head_keys(i, g):
                b = i - BATCH
                act.wait_ge(kh_ready, i + 1)
                if b:
                    act.wait_ge(s_done, BLK * (i - 1) + 7 + g)
                for a in range(4):
                    last = A.activation(Km[:, g, a, :], Kf[:, b % 3, g, CHUNK:CHUNK + TOK], ACT.Copy,
                                        scale=con[:, C_QUAD + a:C_QUAD + a + 1])
                last.then_inc(km_ready, 1)

            def probabilities(i, u):
                if is_a(i):
                    act.wait_ge(zb_ready, i * BLK + u + 1)
                else:
                    act.wait_ge(z_done, i * BLK + u + 1)
                if i >= 1 and u % 4 == 0:
                    act.wait_ge(pv_done, 2 * (i - 1) + u // 4 + 1)
                A.activation(PT[:, u, :], bank[Z_BANK + u % 2][:], ACT.Exp, scale=SCALE).then_inc(p_ready, 1)

            def unnormalised(i, half):
                act.wait_ge(pv_done, 2 * i + half + 1)
                if i:
                    act.wait_ge(t1_done, halves(i - 1) - (0 if is_a(i - 1) else 1 - half))
                w = CH if is_a(i) else BW
                A.activation(OS[:, half, 0:w], bank[O_BANK + half][:, 0:w], ACT.Copy).then_inc(os_ready, 1)

            def normalised(i, half):
                n = (halves(i - 1) if i else 0) + (0 if is_a(i) else half)
                t2 = bank[O_BANK + half]
                act.wait_ge(t2_done, n + 1)
                if i:
                    act.wait_ge(f_done, halves(i - 1) - (0 if is_a(i - 1) else 1 - half))
                A.activation(OT[:, 0 if is_a(i) else half].rearrange("p a b -> p (a b)"), t2[:, 0:2 * P], ACT.Copy).then_inc(ot_ready, 1)

            def query_bias(h):
                act.wait_ge(tq_done, h + 1)
                A.activation(Tq[:, h, :], bank[Z_BANK + h % 2][:, 0:TOEP], ACT.Copy).then_inc(tq_ready, 1)

            squares(0)
            deviation(0)
            projected(0, 0)
            squares(1)
            projected(0, 1)
            projected(0, 2)
            query_bias(0)
            head_queries(0, 0)
            query_bias(1)
            head_queries(0, 1)
            deviation(1)
            squares(2)
            squares(3)
            for t in range(STEPS):
                if t < 3:
                    query_bias(2 * t + 2)
                    query_bias(2 * t + 3)
                if t == 1:
                    deviation(2)
                    A.activation(warm[:, 1:2], eps[:], ACT.Exp)
                if t in (4, 5, 7, 9):
                    weights_b((4, 5, 7, 9).index(t))
                if 0 <= t - LAG < UNITS * BLK:
                    probabilities((t - LAG) // BLK, (t - LAG) % BLK)
                ahead = t + AHEAD
                if ahead < BATCH * BLK:
                    head_queries(ahead // BLK, ahead % BLK)
                for step, when in enumerate((XR_A, Q_A, K_A)):
                    for i in due(t, when, IN_A[1:]):
                        projected(i, step)
                for step, when in enumerate((GV_B + 1, Q_B, K_B)):
                    for i in due(t, when, IN_B):
                        projected(i, step)
                for units, pv, t1, t2, out_step in FINISH:
                    for half in range(2):
                        for i in due(t, t2[half], units_b(units)):
                            normalised(i, half)
                    for i in due(t, t2[1], units_a(units)):
                        normalised(i, 0)
                    for half in range(2):
                        for i in due(t, pv[half], units):
                            unnormalised(i, half)
                for g in range(2):
                    for i in due(t, g - 2, IN_B):
                        head_keys(i, g)


def kernel(x, L0_conv_w_in, L0_conv_w_qk, L0_conv_w_out, L0_conv_rel_bias, L1_conv_w_qkv, L1_conv_w_out):
    import concourse.bacc as bacc
    from concourse.bass_utils import run_bass_kernel_spmd

    nc = bacc.Bacc("TRN2", target_bir_lowering=False, num_devices=1)
    consts, buckets = shape_constants()
    given = {
        "x": np.ascontiguousarray(x).reshape(BATCH, TOK, CH), "w_in": L0_conv_w_in, "w_qk": L0_conv_w_qk,
        "w_outa": L0_conv_w_out, "rel_bias": L0_conv_rel_bias, "w_qkv": L1_conv_w_qkv, "w_outb": L1_conv_w_out,
        "consts": consts, "buckets": buckets,
    }
    arrays = {name: np.ascontiguousarray(a) for name, a in given.items()}
    aps = {name: nc.dram_tensor(name, a.shape, mybir.dt.from_np(a.dtype), kind="ExternalInput").ap() for name, a in arrays.items()}
    out = nc.dram_tensor("y", (BATCH, TOK, CH), F32, kind="ExternalOutput").ap()
    build(nc, out=out, **aps)
    r = run_bass_kernel_spmd(nc, [arrays], core_ids=[0])
    return r.results[0]["y"].reshape(BATCH, HEIGHT, WIDTH, CH)
```
